# Optimizing a Trainium2 kernel written in Bass

```python
import numpy as np
import jax
import jax.numpy as jnp

def _softmax(x, axis=-1):
    return jax.nn.softmax(x, axis=axis)

def _gelu(x):
    return jax.nn.gelu(x, approximate=True)

def _silu(x):
    return jax.nn.silu(x)

def _sigmoid(x):
    return jax.nn.sigmoid(x)

def _layernorm(x, axis=-1, eps=1e-05):
    m = jnp.mean(x, axis=axis, keepdims=True)
    v = jnp.var(x, axis=axis, keepdims=True)
    return (x - m) / jnp.sqrt(v + eps)

def _scatter_add(tgt, idx, src, axis=0):
    return tgt.at[idx].add(src)

def _segment_sum(src, seg, n):
    return jax.ops.segment_sum(src, seg, n)
kernel_name = 'mk_vit_tower_d1_tok_img1024_r4_dc3cf2'

def setup_inputs(seed: int=0):
    np.random.seed(seed)
    _w = jnp.asarray

    def _rec_inputs():
        import jax
        import jax.numpy as jnp
        _rk = jax.random.key(seed)
        x = -0.00016672 + 0.999947 * jax.random.normal(jax.random.fold_in(_rk, 1), (16, 3, 96, 96), jnp.float32)
        return x
    x = _rec_inputs()

    def _L0_tok_setup():
        import jax, jax.numpy as jnp
        import numpy as np
        EPS = 1e-05
        PH = PW = 16

        def _layernorm(x, g, b):
            mu = jnp.mean(x, axis=-1, keepdims=True)
            var = jnp.mean(jnp.square(x - mu), axis=-1, keepdims=True)
            return (x - mu) * jax.lax.rsqrt(var + EPS) * g + b
        key = jax.random.key(seed)
        k1, k2 = jax.random.split(key)
        B, C, H, W_ = (64, 3, 96, 96)
        patch_dim, input_dim = (C * PH * PW, 256)
        img = jax.random.normal(k1, (B, C, H, W_), dtype=jnp.float32)
        W = jax.random.normal(k2, (patch_dim, input_dim), dtype=jnp.float32) * patch_dim ** (-0.5)
        return {'img': img, 'ln1_g': jnp.ones((patch_dim,), jnp.float32), 'ln1_b': jnp.zeros((patch_dim,), jnp.float32), 'W': W, 'b': jnp.zeros((input_dim,), jnp.float32), 'ln2_g': jnp.ones((input_dim,), jnp.float32), 'ln2_b': jnp.zeros((input_dim,), jnp.float32)}
    _L0_tok_all = _L0_tok_setup()
    _L0_tok_in = {k: v for k, v in _L0_tok_all.items() if k in ('ln1_g', 'ln1_b', 'W', 'b', 'ln2_g', 'ln2_b')}
    del _L0_tok_all

    def _L0_attn_setup():
        import jax, jax.numpy as jnp
        import numpy as np
        EMBED_DIM = 256
        NUM_HEADS = 16
        HEAD_DIM = EMBED_DIM // NUM_HEADS
        ALPHA = 1.0

        def _power_law_mask(seq_len, dtype):
            pos = jnp.arange(seq_len)
            delta = pos[None, :] - pos[:, None]
            log_d = jnp.log(jnp.maximum(delta, 0).astype(jnp.float32) + 1.0)
            mask = jnp.where(delta > 0, (-ALPHA * log_d).astype(dtype), jnp.zeros((), dtype))
            mask = jnp.where(delta < 0, jnp.asarray(-jnp.inf, dtype), mask)
            return mask
        key = jax.random.key(seed)
        k1, k2, k3 = jax.random.split(key, 3)
        B, S, D = (2, 512, EMBED_DIM)
        hidden_states = jax.random.normal(k1, (B, S, D), dtype=jnp.float32)
        w_attn = jax.random.normal(k2, (D, 3 * D), dtype=jnp.float32) * D ** (-0.5)
        b_attn = jnp.zeros((3 * D,), dtype=jnp.float32)
        w_proj = jax.random.normal(k3, (D, D), dtype=jnp.float32) * D ** (-0.5)
        b_proj = jnp.zeros((D,), dtype=jnp.float32)
        return {'hidden_states': hidden_states, 'w_attn': w_attn, 'b_attn': b_attn, 'w_proj': w_proj, 'b_proj': b_proj}
    _L0_attn_all = _L0_attn_setup()
    _L0_attn_in = {k: v for k, v in _L0_attn_all.items() if k in ('w_attn', 'b_attn', 'w_proj', 'b_proj')}
    del _L0_attn_all

    def _L0_ffn_setup():
        import jax, jax.numpy as jnp
        import numpy as np
        B, L, D = (4, 128, 256)
        E, TOP_K = (16, 4)
        F = 4 * D
        key = jax.random.key(seed)
        ks = jax.random.split(key, 6)
        scale = 0.02
        return {'x': jax.random.normal(ks[0], (B, L, D), jnp.float32), 'keys': jax.random.normal(ks[1], (E, D), jnp.float32), 'w1': jax.random.normal(ks[2], (E, F, D), jnp.float32) * scale, 'b1': jnp.zeros((E, F), jnp.float32), 'w2': jax.random.normal(ks[3], (E, D, F), jnp.float32) * scale, 'b2': jnp.zeros((E, D), jnp.float32), 'rw': jax.random.normal(ks[4], (E, D), jnp.float32) * scale, 'rb': jnp.zeros((E,), jnp.float32)}
    _L0_ffn_all = _L0_ffn_setup()
    _L0_ffn_in = {k: v for k, v in _L0_ffn_all.items() if k in ('keys', 'w1', 'b1', 'w2', 'b2', 'rw', 'rb')}
    del _L0_ffn_all
    return {'x': x, 'L0_tok_ln1_g': _L0_tok_in['ln1_g'], 'L0_tok_ln1_b': _L0_tok_in['ln1_b'], 'L0_tok_W': _L0_tok_in['W'], 'L0_tok_b': _L0_tok_in['b'], 'L0_tok_ln2_g': _L0_tok_in['ln2_g'], 'L0_tok_ln2_b': _L0_tok_in['ln2_b'], 'L0_attn_w_attn': _L0_attn_in['w_attn'], 'L0_attn_b_attn': _L0_attn_in['b_attn'], 'L0_attn_w_proj': _L0_attn_in['w_proj'], 'L0_attn_b_proj': _L0_attn_in['b_proj'], 'L0_ffn_keys': _L0_ffn_in['keys'], 'L0_ffn_w1': _L0_ffn_in['w1'], 'L0_ffn_b1': _L0_ffn_in['b1'], 'L0_ffn_w2': _L0_ffn_in['w2'], 'L0_ffn_b2': _L0_ffn_in['b2'], 'L0_ffn_rw': _L0_ffn_in['rw'], 'L0_ffn_rb': _L0_ffn_in['rb']}

def reference(x, L0_tok_ln1_g, L0_tok_ln1_b, L0_tok_W, L0_tok_b, L0_tok_ln2_g, L0_tok_ln2_b, L0_attn_w_attn, L0_attn_b_attn, L0_attn_w_proj, L0_attn_b_proj, L0_ffn_keys, L0_ffn_w1, L0_ffn_b1, L0_ffn_w2, L0_ffn_b2, L0_ffn_rw, L0_ffn_rb):
    import jax
    import jax.numpy as jnp

    def _L0_tok_ref(img, ln1_g, ln1_b, W, b, ln2_g, ln2_b):
        import jax, jax.numpy as jnp
        import numpy as np
        EPS = 1e-05
        PH = PW = 16

        def _layernorm(x, g, b):
            mu = jnp.mean(x, axis=-1, keepdims=True)
            var = jnp.mean(jnp.square(x - mu), axis=-1, keepdims=True)
            return (x - mu) * jax.lax.rsqrt(var + EPS) * g + b
        B, C, H, Wd = img.shape
        x = img.reshape(B, C, H // PH, PH, Wd // PW, PW)
        x = jnp.transpose(x, (0, 2, 4, 3, 5, 1))
        x = x.reshape(B, -1, PH * PW * C)
        x = _layernorm(x, ln1_g, ln1_b)
        x = jnp.einsum('bnd,de->bne', x, W) + b
        x = _layernorm(x, ln2_g, ln2_b)
        return x

    def _L0_attn_ref(hidden_states, w_attn, b_attn, w_proj, b_proj):
        import jax, jax.numpy as jnp
        import numpy as np
        EMBED_DIM = 256
        NUM_HEADS = 16
        HEAD_DIM = EMBED_DIM // NUM_HEADS
        ALPHA = 1.0

        def _power_law_mask(seq_len, dtype):
            pos = jnp.arange(seq_len)
            delta = pos[None, :] - pos[:, None]
            log_d = jnp.log(jnp.maximum(delta, 0).astype(jnp.float32) + 1.0)
            mask = jnp.where(delta > 0, (-ALPHA * log_d).astype(dtype), jnp.zeros((), dtype))
            mask = jnp.where(delta < 0, jnp.asarray(-jnp.inf, dtype), mask)
            return mask
        B, S, D = hidden_states.shape
        H, hd = (NUM_HEADS, HEAD_DIM)
        scaling = hd ** (-0.5)
        qkv = hidden_states @ w_attn + b_attn
        q, k, v = jnp.split(qkv, 3, axis=-1)
        q = q.reshape(B, S, H, hd).transpose(0, 2, 1, 3)
        k = k.reshape(B, S, H, hd).transpose(0, 2, 1, 3)
        v = v.reshape(B, S, H, hd).transpose(0, 2, 1, 3)
        scores = jnp.einsum('bhqd,bhkd->bhqk', q, k) * scaling
        scores = scores + _power_law_mask(S, scores.dtype)[None, None]
        attn = jax.nn.softmax(scores, axis=-1)
        out = jnp.einsum('bhqk,bhkd->bhqd', attn, v)
        out = out.transpose(0, 2, 1, 3).reshape(B, S, D)
        out = out @ w_proj + b_proj
        return out

    def _L0_ffn_ref(x, keys, w1, b1, w2, b2, rw, rb):
        import jax, jax.numpy as jnp
        import numpy as np
        B, L, D = (4, 128, 256)
        E, TOP_K = (16, 4)
        F = 4 * D
        diff = x[:, :, None, :] - keys
        dist2 = jnp.sum(diff * diff, axis=-1)
        logits = -dist2 + jnp.einsum('bld,ed->ble', x, rw) + rb
        topv, topi = jax.lax.top_k(logits, TOP_K)
        w = jax.nn.softmax(topv, axis=-1)
        hidden = jax.nn.gelu(jnp.einsum('bld,efd->blef', x, w1) + b1, approximate=False)
        exp_out = jnp.einsum('blef,edf->bled', hidden, w2) + b2
        sel = jnp.take_along_axis(exp_out, topi[..., None], axis=2)
        fused = jnp.sum(w[..., None] * sel, axis=2)
        return fused
    h = _L0_tok_ref(x, L0_tok_ln1_g, L0_tok_ln1_b, L0_tok_W, L0_tok_b, L0_tok_ln2_g, L0_tok_ln2_b)
    h = h + _L0_attn_ref(_layernorm(h, axis=-1), L0_attn_w_attn, L0_attn_b_attn, L0_attn_w_proj, L0_attn_b_proj)
    h = h + _L0_ffn_ref(_layernorm(h, axis=-1), L0_ffn_keys, L0_ffn_w1, L0_ffn_b1, L0_ffn_w2, L0_ffn_b2, L0_ffn_rw, L0_ffn_rb)
    return h

_drawn_inputs = setup_inputs


def setup_inputs(seed=0):
    import zlib

    import numpy as np

    out = dict(_drawn_inputs(seed))
    spreads = {'L0_tok_ln1_g': (1.0, 0.2),
     'L0_tok_ln1_b': (0.0, 0.1),
     'L0_tok_b': (0.0, 0.1),
     'L0_tok_ln2_g': (1.0, 0.2),
     'L0_tok_ln2_b': (0.0, 0.1),
     'L0_attn_b_attn': (0.0, 0.1),
     'L0_attn_b_proj': (0.0, 0.1),
     'L0_ffn_b1': (0.0, 0.277),
     'L0_ffn_b2': (0.0, 0.1),
     'L0_ffn_rb': (0.0, 0.8)}
    factors = {'L0_ffn_rw': 8.0}
    for name, (base, spread) in spreads.items():
        noise = np.random.default_rng([zlib.crc32(name.encode()), seed]).standard_normal(out[name].shape)
        drawn = base * np.exp(spread * noise) if base else spread * noise
        out[name] = jnp.asarray(drawn.astype(out[name].dtype))
    for name, factor in factors.items():
        out[name] = (out[name] * factor).astype(out[name].dtype)
    return out
```

```python
import concourse.bass as bass
from concourse import mybir
from contextlib import ExitStack
import numpy as np

B, C, IMG, PATCH = 16, 3, 96, 16
SIDE = IMG // PATCH
SEQ = SIDE * SIDE
TOK = B * SEQ
P = 128
ROW_TILES = -(-TOK // P)
PAD_TOK = ROW_TILES * P
LAST_ROWS = TOK - (ROW_TILES - 1) * P
PATCH_DIM = C * PATCH * PATCH
PCH = PATCH_DIM // P
D = 256
DCH = D // P
HEADS, HD = 16, 16
HPC = P // HD
SLOT = 64
PAIRS = HEADS // 2
E, TOP_K, F = 16, 4, 1024
FCH = F // P
COPIES = TOK * TOP_K
OVERFLOW_TILES = (COPIES - E) // P
TILES = E + OVERFLOW_TILES
MAX_OVER = -(-TOK // P) - 1
EPS = 1e-5
RING = 3
W1_COLS = DCH * F
W2_COLS = FCH * D

CONSTS = {}
_at = 0
for _name, _n in (("mask", SEQ), ("ident", P), ("before", P), ("headmask", HPC), ("iota_e", E),
                  ("base", E), ("over_at", MAX_OVER), ("tri", E * E), ("iota_o", OVERFLOW_TILES)):
    CONSTS[_name] = (_at, _n)
    _at += _n
CONST_COLS = _at
ROWS = {}
_at = 0
for _name, _n in (("g1", PATCH_DIM), ("b1", PATCH_DIM), ("tok_b", D), ("g2", D), ("b2", D), ("proj_b", D), ("rb", E)):
    ROWS[_name] = (_at, _n)
    _at += _n
ROW_COLS = _at


def const_table():
    t = np.zeros((P, CONST_COLS), np.float32)

    def put(name, value):
        at, n = CONSTS[name]
        t[:, at:at + n] = np.asarray(value, np.float32).reshape(-1, n)
    q = np.arange(P)[:, None] % SLOT
    k = np.arange(SEQ)[None, :]
    m = np.where(k > q, -np.log(np.maximum(k - q, 0) + 1.0), 0.0)
    m = np.where(k < q, -1e30, m)
    m[q[:, 0] >= SEQ] = 0.0
    put("mask", m)
    put("ident", np.eye(P))
    put("before", np.arange(P)[:, None] < np.arange(P)[None, :])
    put("headmask", np.arange(P)[:, None] // HD == np.arange(HPC)[None, :])
    put("iota_e", np.arange(E))
    put("base", np.arange(E) * P)
    put("over_at", (np.arange(MAX_OVER) + 1) * P)
    put("tri", (np.arange(E)[None, :] < np.arange(E)[:, None]).astype(np.float32).reshape(1, -1))
    put("iota_o", np.arange(OVERFLOW_TILES))
    return t


def build(nc, x_tok, consts, rows, bqk, bv, W, wattn, wproj, keysT, rwT, b2, w1, w2, out):
    fp32 = mybir.dt.float32
    u32 = mybir.dt.uint32
    i32 = mybir.dt.int32
    ALU = mybir.AluOpType
    ACT = mybir.ActivationFunctionType
    X = mybir.AxisListType.X

    ctx = ExitStack()
    with ctx:
        def sb(name, shape, dt=fp32):
            return ctx.enter_context(nc.sbuf_tensor(name, shape, dt))

        def sem(name):
            return ctx.enter_context(nc.semaphore(name))

        x_sorted = nc.dram_tensor("x_sorted", (TILES * P, D), fp32, kind="Internal").ap()
        y_sorted = nc.dram_tensor("y_sorted", (TILES * P, D), fp32, kind="Internal").ap()

        const = sb("const", [P, CONST_COLS])
        row = sb("row", [P, ROW_COLS])

        def K(name):
            at, n = CONSTS[name]
            return const[:, at:at + n]

        def R(name):
            at, n = ROWS[name]
            return row[:, at:at + n]

        ident = K("ident")
        bqk_sb = sb("bqk_sb", [P, 4])
        bv_sb = sb("bv_sb", [P, PAIRS, HD])
        W_sb = sb("W_sb", [P, PCH, D])
        wattn_sb = sb("wattn_sb", [P, DCH, 3 * D])
        wproj_sb = sb("wproj_sb", [P, DCH, D])
        keys_sb = sb("keys_sb", [P, DCH, E])
        rw_sb = sb("rw_sb", [P, DCH, E])
        kr = sb("kr", [P, DCH, E])
        nk2 = sb("nk2", [P, DCH, E])
        b2_sb = sb("b2_sb", [E, D])
        ones = sb("ones", [P, P])
        zeros = sb("zeros", [P, D])
        eps = sb("eps", [P, 1])

        x = sb("x", [P, ROW_TILES, PATCH_DIM])
        xT = sb("xT", [P, PCH, PAD_TOK])
        stats = sb("stats", [P, ROW_TILES, 2, 6])
        mv = sb("mv", [P, ROW_TILES, 2])
        sd = sb("sd", [P, ROW_TILES])
        rstd = sb("rstd", [P, ROW_TILES])
        h = sb("h", [P, ROW_TILES, D])
        xa = sb("xa", [P, ROW_TILES, D])
        xaT = sb("xaT", [P, DCH, PAD_TOK])
        Kblk = sb("Kblk", [P, DCH, B, HPC, SEQ])
        Vblk = sb("Vblk", [P, B, PAIRS, 2, HD])
        mx = sb("mx", [P, 2, HEADS])
        Pr = sb("Pr", [P, 2, HEADS, SLOT])
        rs = sb("rs", [P, 2, HEADS])
        PT = sb("PT", [P, PAIRS, P])
        O = sb("O", [P, HEADS, HD])
        OT = sb("OT", [P, DCH, PAD_TOK])
        sq = sb("sq", [P, D])
        x2n = sb("x2n", [P, ROW_TILES])
        L = sb("L", [P, ROW_TILES, E])
        top = sb("top", [P, ROW_TILES, 8])
        topi = sb("topi", [P, ROW_TILES, 8], u32)
        topf = sb("topf", [P, ROW_TILES, TOP_K])
        hot = sb("hot", [P, ROW_TILES, TOP_K, E])
        tmp4 = sb("tmp4", [P, ROW_TILES, TOP_K, E])
        M = sb("M", [P, ROW_TILES, E])
        ew = sb("ew", [P, ROW_TILES, TOP_K])
        es = sb("es", [P, ROW_TILES])
        wk = sb("wk", [P, ROW_TILES, TOP_K])
        Wf = sb("Wf", [P, ROW_TILES, E])
        WT = sb("WT", [E, PAD_TOK])
        over = sb("over", [P, E, MAX_OVER])
        nover = sb("nover", [P, E])
        tri = sb("tri", [P, E, E])
        obase = sb("obase", [P, E])
        oend = sb("oend", [P, E])
        shift = sb("shift", [P, E])
        slot = sb("slot", [P, ROW_TILES, E])
        slotf = sb("slotf", [P, ROW_TILES, TOP_K])
        sloti = sb("sloti", [P, ROW_TILES, TOP_K], u32)
        eidc = sb("eidc", [1, OVERFLOW_TILES, E])
        eidf = sb("eidf", [1, OVERFLOW_TILES])
        eidi = sb("eidi", [1, OVERFLOW_TILES], i32)
        w1_sb = sb("w1_sb", [P, RING, W1_COLS + FCH])
        w2_sb = sb("w2_sb", [P, RING, W2_COLS])
        xspace = xT[:, :, :].rearrange("p c n -> p (c n)")
        QT = xspace[:, 0:DCH * PAD_TOK].rearrange("p (c n) -> p c n", c=DCH)
        KT = xspace[:, 2 * PAD_TOK:3 * PAD_TOK]
        S = xspace[:, 3 * PAD_TOK:3 * PAD_TOK + 2 * HEADS * SEQ].rearrange("p (u a s) -> p u a s", u=2, s=SEQ)
        kspace = Kblk[:, :, :, :, :].rearrange("p c b a s -> p (c b a s)")
        taken = [0]

        def reuse(cols):
            taken[0] += cols
            return kspace[:, taken[0] - cols:taken[0]]

        xg = reuse(RING * D).rearrange("p (k n) -> p k n", k=RING)
        xgT = reuse(RING * D).rearrange("p (k c n) -> p k c n", k=RING, c=DCH)
        hid = reuse(RING * F).rearrange("p (k f n) -> p k f n", k=RING, f=FCH)
        ysb = reuse(RING * D).rearrange("p (k n) -> p k n", k=RING)

        ps = ctx.enter_context(nc.psum_tensor("ps", [P, 8, 512], fp32))

        x_in = [sem(f"x_in{t}") for t in range(ROW_TILES)]
        const_in, row_in, W_in, wattn_in, small_in = (sem(n) for n in ("const_in", "row_in", "W_in", "wattn_in", "small_in"))
        pad_zero, zeros_set, ones_set, eps_set = (sem(n) for n in ("pad_zero", "zeros_set", "ones_set", "eps_set"))
        Vz, Pz, OTz = sem("Vz"), sem("Pz"), sem("OTz")
        dve_step, act_step, pool_step = sem("dve_step"), sem("act_step"), sem("pool_step")
        var_ready, sd_ready = sem("var_ready"), sem("sd_ready")
        xn_ready, xaff_ready = sem("xn_ready"), sem("xaff_ready")
        xT_ps, xT_ready = sem("xT_ps"), sem("xT_ready")
        emb_ps, emb_out = sem("emb_ps"), sem("emb_out")
        xa_ready, xaT_ps, xaT_ready = sem("xa_ready"), sem("xaT_ps"), sem("xaT_ready")
        q_ps, q_ready, k_ps, k_out, kt_ready, kblk_dve, kblk_pool = (
            sem(n) for n in ("q_ps", "q_ready", "k_ps", "k_out", "kt_ready", "kblk_dve", "kblk_pool"))
        v_ps, v_ready = sem("v_ps"), sem("v_ready")
        s_ps, s_out, s_sub, p_ready = sem("s_ps"), sem("s_out"), sem("s_sub"), sem("p_ready")
        pt_ps, pt_ready, o_ps, o_ready, ot_ps, ot_ready = (
            sem(n) for n in ("pt_ps", "pt_ready", "o_ps", "o_ready", "ot_ps", "ot_ready"))
        p_summed = sem("p_summed")
        hb_ready, pr_ps, pr_out = sem("hb_ready"), sem("pr_ps"), sem("pr_out")
        kr_ready, sq_ready = sem("kr_ready"), sem("sq_ready")
        lg_ps, m_ready, dlog_ready, ew_ready = sem("lg_ps"), sem("m_ready"), sem("dlog_ready"), sem("ew_ready")
        pos_ps, cnt_ps, wf_ready, wt_ps, wt_ready, b2_ps = (
            sem(n) for n in ("pos_ps", "cnt_ps", "wf_ready", "wt_ps", "wt_ready", "b2_ps"))
        slot_ready, eid_ready = sem("slot_ready"), sem("eid_ready")
        zero_out, scattered = sem("zero_out"), sem("scattered")
        w1_in = [sem(f"w1_in{k}") for k in range(RING)]
        w2_in = [sem(f"w2_in{k}") for k in range(RING)]
        xg_in = [sem(f"xg_in{k}") for k in range(RING)]
        xgT_ps, xgT_ready = sem("xgT_ps"), sem("xgT_ready")
        up_ps, act_ready = sem("up_ps"), sem("act_ready")
        y_ps, y_ready = sem("y_ps"), sem("y_ready")
        y_stored = [sem(f"y_stored{k}") for k in range(RING)]
        gathered = [sem(f"gathered{t}") for t in range(ROW_TILES)]
        b2_out, out_ready, out_done = sem("b2_out"), sem("out_ready"), sem("out_done")

        block = ctx.enter_context(nc.Block())

        def rows_of(t):
            return P if t < ROW_TILES - 1 else LAST_ROWS

        def expert(ap, e):
            return ap[bass.ds(e, 1), :, :].rearrange("o p n -> (o p) n")

        def tile_rows(ap, i):
            return ap[bass.ds(i * P, P), :]

        def gather_at(t, k):
            n = t * TOP_K + k
            per = ROW_TILES * PATCH_DIM // D
            if n < per:
                return x[:, :, :].rearrange("p t n -> p (t n)")[:, n * D:(n + 1) * D]
            n -= per
            return xT[:, :, :].rearrange("p t n -> p (t n)")[:, n * D:(n + 1) * D]

        @block.sync
        def _(sp):
            for t in range(ROW_TILES):
                sp.dma_start(x[0:rows_of(t), t, :], x_tok[t * P:t * P + rows_of(t), :]).then_inc(x_in[t], 16)
            sp.dma_start(W_sb[:, :, :], W.rearrange("(c p) n -> p c n", p=P)).then_inc(W_in, 16)
            sp.dma_start(wattn_sb[:, :, :], wattn.rearrange("(c p) n -> p c n", p=P)).then_inc(wattn_in, 16)
            for i in range(RING):
                sp.dma_start(w1_sb[:, i, :], w1[i, :, :]).then_inc(w1_in[i], 16)
                sp.dma_start(w2_sb[:, i, :], w2[i, :, :]).then_inc(w2_in[i], 16)
            sp.wait_ge(zeros_set, 1)
            sp.dma_start(x_sorted.rearrange("(t p) n -> p t n", p=P),
                         zeros[:, None, :].broadcast_to([P, TILES, D])).then_inc(zero_out, 16)
            sp.wait_ge(scattered, 16 * ROW_TILES * TOP_K)
            for i in range(RING):
                sp.dma_start(xg[:, i, :], x_sorted[i * P:(i + 1) * P, :]).then_inc(xg_in[i], 16)

            def load(i, k, e):
                sp.wait_ge(act_ready, 2 * (i - (RING - 1)))
                sp.dma_start(w1_sb[:, k, :], expert(w1, e)).then_inc(w1_in[k], 16)
                sp.wait_ge(xgT_ps, i - (RING - 1))
                sp.dma_start(xg[:, k, :], tile_rows(x_sorted, i)).then_inc(xg_in[k], 16)
                sp.wait_ge(y_ps, i - (RING - 1))
                sp.dma_start(w2_sb[:, k, :], expert(w2, e)).then_inc(w2_in[k], 16)

            last = E - E % RING
            with sp.Fori(1, last // RING) as r:
                for k in range(RING):
                    load(r * RING + k, k, r * RING + k)
            for i in range(last, E):
                load(i, i % RING, i)
            sp.wait_ge(eid_ready, 1)

            def overflow(i, k):
                e = sp.value_load(eidi[0:1, bass.ds(i - E, 1)], min_val=0, max_val=E - 1)
                load(i, k, e)

            first = -(-E // RING) * RING
            for i in range(E, first):
                overflow(i, i % RING)
            with sp.Fori(first // RING, TILES // RING) as r:
                for k in range(RING):
                    overflow(r * RING + k, k)
            for t in range(ROW_TILES):
                sp.wait_ge(out_ready, t + 1)
                sp.dma_start(out[t * P:t * P + rows_of(t), :], h[0:rows_of(t), t, :]).then_inc(out_done, 16)
            sp.wait_ge(out_done, 16 * ROW_TILES)

        @block.gpsimd
        def _(pool):
            nc.gpsimd.memset(x[LAST_ROWS:P, ROW_TILES - 1, :], 0.0).then_inc(pad_zero, 1)
            pool.wait_ge(pad_zero, 1)
            nc.gpsimd.memset(zeros[:, :], 0.0).then_inc(zeros_set, 1)
            nc.gpsimd.memset(Pr[:, :, :, :], 0.0).then_inc(Pz, 1)
            nc.gpsimd.memset(OT[:, :, TOK:PAD_TOK], 0.0).then_inc(OTz, 1)
            pool.wait_ge(row_in, 16)
            for t in range(ROW_TILES):
                pool.wait_ge(xn_ready, t + 1)
                nc.gpsimd.tensor_tensor(x[:, t, :], x[:, t, :], R("g1"), ALU.mult).then_inc(pool_step, 1)
                pool.wait_ge(pool_step, t + 1)
                nc.gpsimd.tensor_tensor(x[:, t, :], x[:, t, :], R("b1"), ALU.add).then_inc(xaff_ready, 1)
            nc.gpsimd.memset(Vblk[:, :, :, :, :], 0.0).then_inc(Vz, 1)
            pool.wait_ge(const_in, 16)
            for half in range(2):
                pool.wait_ge(kt_ready, half + 1)
                kk = KT[:, half * TOK // 2:(half + 1) * TOK // 2].rearrange("p (b s) -> p b s", s=SEQ)
                for hh in range(HPC):
                    o = nc.gpsimd.tensor_scalar(Kblk[:, 1, half * B // 2:(half + 1) * B // 2, hh, :], kk,
                                                K("headmask")[:, hh:hh + 1], None, ALU.mult)
                o.then_inc(kblk_pool, 1)
            pool.wait_ge(xa_ready, 1)
            nc.gpsimd.tensor_tensor(h[:, :, :], h[:, :, :],
                                    R("proj_b")[:, None, :].broadcast_to([P, ROW_TILES, D]), ALU.add).then_inc(hb_ready, 1)
            pool.wait_ge(slot_ready, 1)
            pool.wait_ge(zero_out, 16)
            for t in range(ROW_TILES):
                n = rows_of(t)
                for k in range(TOP_K):
                    pool.indirect_dma_start(
                        out=x_sorted[:, :], out_offset=bass.IndirectOffsetOnAxis(ap=sloti[0:n, t, k:k + 1], axis=0),
                        in_=xa[0:n, t, :], in_offset=None).then_inc(scattered, 16)
            for k in range(RING):
                pool.wait_ge(y_stored[k], 16 * len(range(k, TILES, RING)))
            for t in range(ROW_TILES):
                n = rows_of(t)
                for k in range(TOP_K):
                    dst = gather_at(t, k)
                    pool.indirect_dma_start(
                        out=dst[0:n, :], out_offset=None, in_=y_sorted[:, :],
                        in_offset=bass.IndirectOffsetOnAxis(ap=sloti[0:n, t, k:k + 1], axis=0)).then_inc(gathered[t], 16)

        @block.scalar
        def _(act):
            act.dma_start(row[:, :], rows.partition_broadcast(P) if rows.ndim == 1 else rows).then_inc(row_in, 16)
            act.dma_start(const[:, :], consts).then_inc(const_in, 16)
            act.dma_start(wproj_sb[:, :, :], wproj.rearrange("(c p) n -> p c n", p=P)).then_inc(small_in, 16)
            act.dma_start(keys_sb[:, :, :], keysT.rearrange("(c p) n -> p c n", p=P)).then_inc(small_in, 16)
            act.dma_start(rw_sb[:, :, :], rwT.rearrange("(c p) n -> p c n", p=P)).then_inc(small_in, 16)
            act.dma_start(b2_sb[:, :], b2).then_inc(small_in, 16)
            act.dma_start(bqk_sb[:, :], bqk).then_inc(small_in, 16)
            for j in range(2):
                act.dma_start(bv_sb[j * SLOT:(j + 1) * SLOT, :, :].rearrange("p a n -> p (a n)"),
                              bv[j, :].partition_broadcast(SLOT)).then_inc(small_in, 16)

            def std(tiles, n):
                act.wait_ge(var_ready, n)
                nc.scalar.activation(sd[:, tiles], mv[:, tiles, 1], ACT.Sqrt, bias=eps[:, 0:1]).then_inc(sd_ready, 1)

            act.wait_ge(eps_set, 1)

            def copy_xT(t):
                act.wait_ge(xT_ps, t + 1)
                bank = 2 * (t % 2)
                nc.scalar.copy(xT[:, 0:3, t * P:(t + 1) * P],
                               ps[:, bank, 0:3 * P].rearrange("p (c n) -> p c n", n=P))
                nc.scalar.copy(xT[:, 3:6, t * P:(t + 1) * P],
                               ps[:, bank + 1, 0:3 * P].rearrange("p (c n) -> p c n", n=P)).then_inc(xT_ready, 1)

            std(slice(0, 1), 1)
            for t in range(1, ROW_TILES):
                std(slice(t, t + 1), t + 1)
                copy_xT(t - 1)
            copy_xT(ROW_TILES - 1)
            std(slice(0, ROW_TILES), ROW_TILES + 1)
            std(slice(0, ROW_TILES), ROW_TILES + 2)

            def copy_rowsT(n):
                act.wait_ge(xaT_ps, n)
                for c in range(DCH):
                    nc.scalar.copy(xaT[:, c, 0:4 * P], ps[:, 2 * c, :])
                    o = nc.scalar.copy(xaT[:, c, 4 * P:PAD_TOK], ps[:, 2 * c + 1, 0:P])
                o.then_inc(xaT_ready, 1)

            copy_rowsT(1)
            act.wait_ge(small_in, 16 * 7)
            for m in range(2):
                for half in range(2):
                    act.wait_ge(q_ps, 2 * m + half + 1)
                    n = TOK // 2 + 32 * half
                    nc.scalar.activation(QT[:, m, half * TOK // 2:half * TOK // 2 + n], ps[:, 2 * m + half, 0:n],
                                         ACT.Identity, bias=bqk_sb[:, m:m + 1]).then_inc(q_ready, 1)
            for half in range(2):
                act.wait_ge(k_ps, 3 + half)
                nc.scalar.activation(KT[:, half * TOK // 2:(half + 1) * TOK // 2], ps[:, 6 + half, 0:TOK // 2],
                                     ACT.Identity, bias=bqk_sb[:, 3:4]).then_inc(kt_ready, 1)
            act.wait_ge(Pz, 1)
            act.wait_ge(OTz, 1)

            def softmax_exp(t):
                act.wait_ge(s_sub, t + 1)
                if t >= 2:
                    act.wait_ge(pt_ps, t - 1)
                    act.wait_ge(p_summed, t - 1)
                nc.scalar.activation(Pr[:, t % 2, :, 0:SEQ], S[:, t % 2, :, :], ACT.Exp).then_inc(p_ready, 1)

            softmax_exp(0)
            for t in range(B // 2):
                act.wait_ge(pt_ps, t + 1)
                if t >= 1:
                    act.wait_ge(o_ps, t)
                nc.scalar.copy(PT[:, 0:PAIRS // 2, :], ps[:, 4, :].rearrange("p (a n) -> p a n", n=P))
                nc.scalar.copy(PT[:, PAIRS // 2:, :], ps[:, 5, :].rearrange("p (a n) -> p a n", n=P)).then_inc(pt_ready, 1)
                if t + 1 < B // 2:
                    softmax_exp(t + 1)
                act.wait_ge(ot_ps, t + 1)
                nc.scalar.copy(OT[:, :, t * 2 * SEQ:(t + 1) * 2 * SEQ].rearrange("p c (j s) -> p c j s", s=SEQ),
                               ps[:, 7, 0:2 * P].rearrange("p (c j s) -> p c j s", c=DCH, s=SLOT)[:, :, :, 0:SEQ]).then_inc(ot_ready, 1)
            std(slice(0, ROW_TILES), ROW_TILES + 3)
            act.wait_ge(xa_ready, 2)
            for t in range(ROW_TILES):
                o = nc.scalar.activation(sq[:, :], xa[:, t, :], ACT.Square, accum_out=x2n[:, t:t + 1])
                o.then_inc(act_step, 1)
                act.wait_ge(act_step, t + 1)
            o = nc.scalar.copy(sq[:, 0:1], x2n[:, 0:1]).then_inc(sq_ready, 1)
            copy_rowsT(2)
            act.wait_ge(dlog_ready, 1)
            nc.scalar.activation(ew[:, :, :], topf[:, :, :], ACT.Exp).then_inc(ew_ready, 1)
            act.wait_ge(wt_ps, 1)
            nc.scalar.copy(WT[:, 0:4 * P], ps[0:E, 4, :])
            nc.scalar.copy(WT[:, 4 * P:PAD_TOK], ps[0:E, 5, 0:P]).then_inc(wt_ready, 1)

            def gelu_tile(i, k):
                for half in range(2):
                    act.wait_ge(up_ps, 2 * i + half + 1)
                    for f in range(FCH // 2):
                        fc = half * FCH // 2 + f
                        o = nc.scalar.activation(hid[:, k, fc, :], ps[:, 2 * k + half, f * P:(f + 1) * P], ACT.Gelu,
                                                 bias=w1_sb[:, k, W1_COLS + fc:W1_COLS + fc + 1])
                    o.then_inc(act_ready, 1)

            def store_y(i, k):
                act.wait_ge(y_ready, i + 1)
                act.dma_start(tile_rows(y_sorted, i), ysb[:, k, :]).then_inc(y_stored[k], 16)

            gelu_tile(0, 0)
            gelu_tile(1, 1)
            store_y(0, 0)
            gelu_tile(2, 2)
            store_y(1, 1)
            with act.Fori(1, TILES // RING) as r:
                for k in range(RING):
                    gelu_tile(r * RING + k, k)
                    store_y(r * RING + k - 1, (k - 1) % RING)
            store_y(TILES - 1, (TILES - 1) % RING)

        @block.vector
        def _(dve):
            steps = [0]

            def link(ins):
                steps[0] += 1
                ins.then_inc(dve_step, 1)
                dve.wait_ge(dve_step, steps[0])

            V = nc.vector
            V.memset(eps[:, :], EPS).then_inc(eps_set, 1)
            V.memset(ones[:, :], 1.0).then_inc(ones_set, 1)

            def rows_stats(t, src, width):
                parts = -(-width // 512)
                n = width // parts
                for j in range(parts):
                    link(V.bn_stats(stats[:, t, j, :], src[:, j * n:(j + 1) * n]))
                return V.bn_aggr(mv[:, t, :], stats[:, t, 0:parts, :].rearrange("p a b -> p (a b)"))

            def norm(dst, src, t):
                return V.tensor_scalar(dst, src, mv[:, t, 0:1], rstd[:, t:t + 1], ALU.subtract, ALU.mult)

            for t in range(ROW_TILES + 1):
                if t < ROW_TILES:
                    dve.wait_ge(x_in[t], 16)
                    if t == ROW_TILES - 1:
                        dve.wait_ge(pad_zero, 1)
                    rows_stats(t, x[:, t, :], PATCH_DIM).then_inc(var_ready, 1)
                    dve.wait_ge(var_ready, t + 1)
                if t >= 1:
                    dve.wait_ge(sd_ready, t)
                    link(V.reciprocal(rstd[:, t - 1:t], sd[:, t - 1:t]))
                    norm(x[:, t - 1, :], x[:, t - 1, :], t - 1).then_inc(xn_ready, 1)

            def layernorm(dst, n):
                for t in range(ROW_TILES):
                    o = rows_stats(t, h[:, t, :], D)
                    if t < ROW_TILES - 1:
                        link(o)
                o.then_inc(var_ready, 1)
                dve.wait_ge(sd_ready, n)
                link(V.reciprocal(rstd[:, :], sd[:, :]))
                for t in range(ROW_TILES):
                    o = norm(dst[:, t, :], h[:, t, :], t)
                return o

            dve.wait_ge(row_in, 16)
            for t in range(ROW_TILES):
                dve.wait_ge(emb_ps, t + 1)
                V.tensor_tensor(h[:, t, :], ps[:, 4 + t % 4, 0:D], R("tok_b"), ALU.add).then_inc(emb_out, 1)
            dve.wait_ge(emb_out, ROW_TILES)
            link(layernorm(h, ROW_TILES + 1))
            g2 = R("g2")[:, None, :].broadcast_to([P, ROW_TILES, D])
            b2r = R("b2")[:, None, :].broadcast_to([P, ROW_TILES, D])
            link(V.tensor_tensor(h[:, :, :], h[:, :, :], g2, ALU.mult))
            link(V.tensor_tensor(h[:, :, :], h[:, :, :], b2r, ALU.add))
            layernorm(xa, ROW_TILES + 2).then_inc(xa_ready, 1)

            dve.wait_ge(small_in, 16 * 7)
            V.scalar_tensor_tensor(out=kr[:, :, :], in0=keys_sb[:, :, :], scalar=2.0, in1=rw_sb[:, :, :],
                                   op0=ALU.mult, op1=ALU.add)
            V.scalar_tensor_tensor(out=nk2[:, :, :], in0=keys_sb[:, :, :], scalar=-1.0, in1=keys_sb[:, :, :],
                                   op0=ALU.mult, op1=ALU.mult).then_inc(kr_ready, 1)
            dve.wait_ge(const_in, 16)
            for half in range(2):
                dve.wait_ge(k_ps, half + 1)
                kk = ps[:, 4 + half, 0:TOK // 2].rearrange("p (b s) -> p b s", s=SEQ)
                for hh in range(HPC):
                    o = V.tensor_scalar(Kblk[:, 0, half * B // 2:(half + 1) * B // 2, hh, :], kk, bqk_sb[:, 2:3],
                                        K("headmask")[:, hh:hh + 1], ALU.add, ALU.mult)
                o.then_inc(kblk_dve, 1)
            dve.wait_ge(Vz, 1)
            for g in range(4):
                dve.wait_ge(v_ps, g + 1)
                for j in range(2):
                    lo = j * SLOT
                    o = V.tensor_tensor(
                        Vblk[lo:lo + SLOT, 4 * g:4 * g + 4, :, j, :],
                        ps[lo:lo + SLOT, g, :].rearrange("p (b a n) -> p b a n", b=4, n=HD),
                        bv_sb[lo:lo + SLOT, None, :, :].broadcast_to([SLOT, 4, PAIRS, HD]), ALU.add)
                    if j == 0:
                        link(o)
                o.then_inc(v_ready, 1)

            mask = K("mask")[:, None, :].broadcast_to([P, HPC, SEQ])

            def scores(t):
                u = t % 2
                dve.wait_ge(s_ps, t + 1)
                if t >= 2:
                    dve.wait_ge(p_ready, t - 1)
                for c in range(DCH):
                    o = V.scalar_tensor_tensor(
                        out=S[:, u, c * HPC:(c + 1) * HPC, :],
                        in0=ps[:, 2 * u + c, 0:HPC * SEQ].rearrange("p (a s) -> p a s", s=SEQ),
                        scalar=HD ** -0.5, in1=mask, op0=ALU.mult, op1=ALU.add)
                o.then_inc(s_out, 1)
                dve.wait_ge(s_out, t + 1)
                link(V.tensor_reduce(mx[:, u, :], S[:, u, :, :], X, ALU.max))
                V.tensor_tensor(S[:, u, :, :], S[:, u, :, :],
                                mx[:, u, :, None].broadcast_to([P, HEADS, SEQ]), ALU.subtract).then_inc(s_sub, 1)

            scores(0)
            for t in range(B // 2):
                if t + 1 < B // 2:
                    scores(t + 1)
                u = t % 2
                dve.wait_ge(p_ready, t + 1)
                V.tensor_reduce(rs[:, u, :], Pr[:, u, :, 0:SEQ], X, ALU.add).then_inc(p_summed, 1)
                dve.wait_ge(p_summed, t + 1)
                link(V.reciprocal(rs[:, u, :], rs[:, u, :]))
                dve.wait_ge(o_ps, t + 1)
                if t >= 1:
                    dve.wait_ge(ot_ps, t)
                V.tensor_tensor(O[:, :, :], ps[:, 6, 0:D].rearrange("p (a n) -> p a n", n=HD),
                                rs[:, u, :, None].broadcast_to([P, HEADS, HD]), ALU.mult).then_inc(o_ready, 1)

            dve.wait_ge(hb_ready, 1)
            for t in range(ROW_TILES):
                dve.wait_ge(pr_ps, t + 1)
                V.tensor_tensor(h[:, t, :], h[:, t, :], ps[:, t, 0:D], ALU.add).then_inc(pr_out, 1)
            dve.wait_ge(pr_out, ROW_TILES)
            layernorm(xa, ROW_TILES + 3).then_inc(xa_ready, 1)

            dve.wait_ge(lg_ps, 1)
            dve.wait_ge(sq_ready, 1)
            link(V.tensor_tensor(L[:, :, :], ps[:, 6, 0:ROW_TILES * E].rearrange("p (t e) -> p t e", e=E),
                                 R("rb")[:, None, :].broadcast_to([P, ROW_TILES, E]), ALU.add))
            link(V.tensor_tensor(L[:, :, :], L[:, :, :], x2n[:, :, None].broadcast_to([P, ROW_TILES, E]), ALU.subtract))
            for t in range(ROW_TILES):
                o = V.max(top[:, t, :], L[:, t, :])
            link(o)
            for t in range(ROW_TILES):
                o = V.max_index(topi[:, t, :], top[:, t, :], L[:, t, :])
            link(o)
            link(V.tensor_copy(topf[:, :, :], topi[:, :, 0:TOP_K]))
            e4 = [P, ROW_TILES, TOP_K, E]
            link(V.tensor_tensor(hot[:, :, :, :], topf[:, :, :, None].broadcast_to(e4),
                                 K("iota_e")[:, None, None, :].broadcast_to(e4), ALU.is_equal))
            V.tensor_reduce(M[:, :, :], hot[:, :, :, :].rearrange("p t k e -> p t e k"), X, ALU.add).then_inc(m_ready, 1)
            V.tensor_tensor(topf[:, :, :], top[:, :, 0:TOP_K],
                            top[:, :, 0:1].broadcast_to([P, ROW_TILES, TOP_K]), ALU.subtract).then_inc(dlog_ready, 1)
            dve.wait_ge(cnt_ps, 1)
            cnt = ps[:, 7, 256:256 + E]
            link(V.tensor_tensor(over[:, :, :], cnt[:, :, None].broadcast_to([P, E, MAX_OVER]),
                                 K("over_at")[:, None, :].broadcast_to([P, E, MAX_OVER]), ALU.is_gt))
            link(V.tensor_reduce(nover[:, :], over[:, :, :], X, ALU.add))
            link(V.tensor_tensor(tri[:, :, :], K("tri").rearrange("p (a b) -> p a b", b=E),
                                 nover[:, None, :].broadcast_to([P, E, E]), ALU.mult))
            link(V.tensor_reduce(obase[:, :], tri[:, :, :], X, ALU.add))
            link(V.tensor_tensor(oend[:, :], obase[:, :], nover[:, :], ALU.add))
            link(V.tensor_scalar(shift[:, :], obase[:, :], float(P), float((E - 1) * P), ALU.mult, ALU.add))
            link(V.tensor_tensor(shift[:, :], shift[:, :], K("base"), ALU.subtract))
            et = [P, ROW_TILES, E]
            pos = ps[:, 7, 0:ROW_TILES * E].rearrange("p (t e) -> p t e", e=E)
            link(V.scalar_tensor_tensor(out=slot[:, :, :], in0=pos, scalar=float(P),
                                        in1=shift[:, None, :].broadcast_to(et), op0=ALU.is_ge, op1=ALU.mult))
            link(V.tensor_tensor(slot[:, :, :], slot[:, :, :], K("base")[:, None, :].broadcast_to(et), ALU.add))
            link(V.tensor_tensor(slot[:, :, :], slot[:, :, :], pos, ALU.add))
            link(V.tensor_tensor(tmp4[:, :, :, :], hot[:, :, :, :], slot[:, :, None, :].broadcast_to(e4), ALU.mult))
            link(V.tensor_reduce(slotf[:, :, :], tmp4[:, :, :, :], X, ALU.add))
            V.tensor_copy(sloti[:, :, :], slotf[:, :, :]).then_inc(slot_ready, 1)
            eo = [1, OVERFLOW_TILES, E]
            link(V.tensor_tensor(eidc[:, :, :], oend[0:1, None, :].broadcast_to(eo),
                                 K("iota_o")[0:1, :, None].broadcast_to(eo), ALU.is_le))
            link(V.tensor_reduce(eidf[:, :], eidc[:, :, :], X, ALU.add))
            link(V.tensor_scalar(eidf[:, :], eidf[:, :], float(E - 1), None, ALU.min))
            V.tensor_copy(eidi[:, :], eidf[:, :]).then_inc(eid_ready, 1)
            dve.wait_ge(ew_ready, 1)
            link(V.tensor_reduce(es[:, :], ew[:, :, :], X, ALU.add))
            link(V.reciprocal(es[:, :], es[:, :]))
            link(V.tensor_tensor(wk[:, :, :], ew[:, :, :], es[:, :, None].broadcast_to([P, ROW_TILES, TOP_K]), ALU.mult))
            link(V.tensor_tensor(tmp4[:, :, :, :], hot[:, :, :, :], wk[:, :, :, None].broadcast_to(e4), ALU.mult))
            V.tensor_reduce(Wf[:, :, :], tmp4[:, :, :, :].rearrange("p t k e -> p t e k"), X, ALU.add).then_inc(wf_ready, 1)
            for t in range(ROW_TILES):
                dve.wait_ge(b2_ps, t + 1)
                V.tensor_tensor(h[:, t, :], h[:, t, :], ps[:, t, 0:D], ALU.add).then_inc(b2_out, 1)

            def take_xT(i, k):
                dve.wait_ge(xgT_ps, i + 1)
                V.tensor_copy(xgT[:, k, :, :], ps[:, 6, 0:D].rearrange("p (c n) -> p c n", n=P)).then_inc(xgT_ready, 1)

            def take_y(i, k, reused):
                dve.wait_ge(y_ps, i + 1)
                if reused is not None:
                    dve.wait_ge(y_stored[k], 16 * reused)
                V.tensor_copy(ysb[:, k, :], ps[:, 7, 0:D]).then_inc(y_ready, 1)

            take_xT(0, 0)
            for i in range(RING):
                take_xT(i + 1, (i + 1) % RING)
                take_y(i, i, None)
            with dve.Fori(1, TILES // RING - 1) as r:
                for k in range(RING):
                    take_xT(r * RING + k + 1, (k + 1) % RING)
                    take_y(r * RING + k, k, r)
            for i in range(TILES - RING, TILES):
                if i + 1 < TILES:
                    take_xT(i + 1, (i + 1) % RING)
                take_y(i, i % RING, i // RING)

            dve.wait_ge(b2_out, ROW_TILES)
            for t in range(ROW_TILES):
                dve.wait_ge(gathered[t], 16 * TOP_K)
                n = rows_of(t)
                for k in range(TOP_K):
                    o = V.scalar_tensor_tensor(out=h[0:n, t, :], in0=gather_at(t, k)[0:n, :], scalar=wk[0:n, t, k:k + 1],
                                               in1=h[0:n, t, :], op0=ALU.mult, op1=ALU.add)
                    if k < TOP_K - 1:
                        link(o)
                o.then_inc(out_ready, 1)

        @block.tensor
        def _(pe):
            mm = nc.tensor.matmul
            pe.wait_ge(const_in, 16)

            def embed(t):
                pe.wait_ge(xT_ready, t + 1)
                if t == 0:
                    pe.wait_ge(W_in, 16)
                if t >= 4:
                    pe.wait_ge(emb_out, t - 3)
                for c in range(PCH):
                    o = mm(ps[:, 4 + t % 4, 0:D], xT[:, c, t * P:(t + 1) * P], W_sb[:, c, :], start=(c == 0), stop=(c == PCH - 1))
                o.then_inc(emb_ps, 1)

            for t in range(ROW_TILES):
                pe.wait_ge(xaff_ready, t + 1)
                if t >= 2:
                    pe.wait_ge(xT_ready, t - 1)
                for c in range(PCH):
                    o = nc.tensor.transpose(ps[:, 2 * (t % 2) + c // 3, (c % 3) * P:(c % 3 + 1) * P],
                                            x[:, t, c * P:(c + 1) * P], ident)
                o.then_inc(xT_ps, 1)
                if t >= 1:
                    embed(t - 1)
            embed(ROW_TILES - 1)

            def rowsT(n):
                pe.wait_ge(xa_ready, n)
                for c in range(DCH):
                    for t in range(ROW_TILES):
                        o = nc.tensor.transpose(ps[:, 2 * c + t // 4, (t % 4) * P:(t % 4 + 1) * P],
                                                xa[:, t, c * P:(c + 1) * P], ident)
                o.then_inc(xaT_ps, 1)

            rowsT(1)
            pe.wait_ge(xaT_ready, 1)
            pe.wait_ge(wattn_in, 16)
            pe.wait_ge(emb_out, ROW_TILES)
            for m in range(4):
                for half in range(2):
                    n = TOK // 2 + (32 * half if m < 2 else 0)
                    for c in range(DCH):
                        o = mm(ps[:, 2 * m + half, 0:n], wattn_sb[:, c, m * P:(m + 1) * P],
                               xaT[:, c, half * TOK // 2:half * TOK // 2 + n], start=(c == 0), stop=(c == DCH - 1))
                    o.then_inc(q_ps if m < 2 else k_ps, 1)
            for g in range(4):
                pe.wait_ge(q_ready, g + 1)
                for b in range(4 * g, 4 * g + 4):
                    for j in range(2):
                        for c in range(DCH):
                            wv = wattn_sb[:, c, 2 * D:3 * D].rearrange("p (a j n) -> p a j n", j=2, n=HD)[:, :, j, :]
                            o = mm(ps[j * SLOT:(j + 1) * SLOT, g, (b % 4) * P:(b % 4 + 1) * P],
                                   xaT[:, c, b * SEQ:b * SEQ + SLOT], wv, start=(c == 0), stop=(c == DCH - 1))
                o.then_inc(v_ps, 1)

            def scores(t):
                if t == 0:
                    pe.wait_ge(kblk_dve, 2)
                    pe.wait_ge(kblk_pool, 2)
                    pe.wait_ge(v_ready, 2)
                    pe.wait_ge(q_ready, 4)
                if t == 1:
                    pe.wait_ge(v_ready, 4)
                if t >= 2:
                    pe.wait_ge(s_out, t - 1)
                for c in range(DCH):
                    for j in range(2):
                        b = 2 * t + j
                        o = mm(ps[j * SLOT:(j + 1) * SLOT, 2 * (t % 2) + c, 0:HPC * SEQ],
                               QT[:, c, b * SEQ:b * SEQ + SLOT], Kblk[:, c, b, :, :].rearrange("p a s -> p (a s)"),
                               start=True, stop=True)
                o.then_inc(s_ps, 1)

            def probsT(t):
                pe.wait_ge(p_ready, t + 1)
                if t >= 1:
                    pe.wait_ge(pt_ready, t)
                for a in range(PAIRS):
                    o = nc.tensor.transpose(ps[:, 4 + a // 4, (a % 4) * P:(a % 4 + 1) * P],
                                            Pr[:, t % 2, 2 * a:2 * a + 2, :].rearrange("p a s -> p (a s)"), ident)
                o.then_inc(pt_ps, 1)

            def attend(t):
                pe.wait_ge(pt_ready, t + 1)
                pe.wait_ge(v_ready, 4)
                if t >= 1:
                    pe.wait_ge(o_ready, t)
                for j in range(2):
                    for a in range(PAIRS):
                        o = mm(ps[j * SLOT:(j + 1) * SLOT, 6, a * 2 * HD:(a + 1) * 2 * HD],
                               PT[:, a, j * SLOT:(j + 1) * SLOT],
                               Vblk[:, 2 * t + j, a, :, :].rearrange("p j n -> p (j n)"), start=True, stop=True)
                o.then_inc(o_ps, 1)

            def outT(t):
                pe.wait_ge(o_ready, t + 1)
                if t >= 1:
                    pe.wait_ge(ot_ready, t)
                for c in range(DCH):
                    o = nc.tensor.transpose(ps[:, 7, c * P:(c + 1) * P],
                                            O[:, c * HPC:(c + 1) * HPC, :].rearrange("p a n -> p (a n)"), ident)
                o.then_inc(ot_ps, 1)

            scores(0)
            for t in range(B // 2):
                if t + 1 < B // 2:
                    scores(t + 1)
                probsT(t)
                attend(t)
                outT(t)
            pe.wait_ge(small_in, 16 * 7)
            pe.wait_ge(ot_ready, B // 2)
            for t in range(ROW_TILES):
                if t == 0:
                    pe.wait_ge(s_out, B // 2)
                for c in range(DCH):
                    o = mm(ps[:, t, 0:D], OT[:, c, t * P:(t + 1) * P], wproj_sb[:, c, :], start=(c == 0), stop=(c == DCH - 1))
                o.then_inc(pr_ps, 1)
            rowsT(2)
            pe.wait_ge(xaT_ready, 2)
            pe.wait_ge(kr_ready, 1)
            pe.wait_ge(ones_set, 1)
            for t in range(ROW_TILES):
                for c in range(DCH):
                    mm(ps[:, 6, t * E:(t + 1) * E], xaT[:, c, t * P:(t + 1) * P], kr[:, c, :], start=(c == 0), stop=False)
                for c in range(DCH):
                    o = mm(ps[:, 6, t * E:(t + 1) * E], ones[:, :], nk2[:, c, :], start=False, stop=(c == DCH - 1))
            o.then_inc(lg_ps, 1)
            pe.wait_ge(m_ready, 1)
            for t in range(ROW_TILES):
                n = rows_of(t)
                for s in range(t):
                    mm(ps[:, 7, t * E:(t + 1) * E], ones[:, :], M[:, s, :], start=(s == 0), stop=False)
                o = mm(ps[:, 7, t * E:(t + 1) * E], K("before")[0:n, :], M[0:n, t, :], start=(t == 0), stop=True)
            o.then_inc(pos_ps, 1)
            for t in range(ROW_TILES):
                n = rows_of(t)
                o = mm(ps[:, 7, 256:256 + E], ones[0:n, :], M[0:n, t, :], start=(t == 0), stop=(t == ROW_TILES - 1))
            o.then_inc(cnt_ps, 1)
            pe.wait_ge(wf_ready, 1)
            for t in range(ROW_TILES):
                o = nc.tensor.transpose(ps[0:E, 4 + t // 4, (t % 4) * P:(t % 4 + 1) * P], Wf[:, t, :], ident)
            o.then_inc(wt_ps, 1)
            pe.wait_ge(wt_ready, 1)
            for t in range(ROW_TILES):
                mm(ps[:, t, 0:D], WT[:, t * P:(t + 1) * P], b2_sb[:, :], start=True, stop=True).then_inc(b2_ps, 1)

            def tileT(i, k, n_in):
                pe.wait_ge(xg_in[k], 16 * n_in)
                for c in range(DCH):
                    o = nc.tensor.transpose(ps[:, 6, c * P:(c + 1) * P], xg[:, k, c * P:(c + 1) * P], ident)
                o.then_inc(xgT_ps, 1)

            def up(i, k, n_in):
                pe.wait_ge(w1_in[k], 16 * n_in)
                pe.wait_ge(xgT_ready, i + 1)
                for half in range(2):
                    for f in range(FCH // 2):
                        fc = half * FCH // 2 + f
                        for c in range(DCH):
                            o = mm(ps[:, 2 * k + half, f * P:(f + 1) * P],
                                   w1_sb[:, k, c * F + fc * P:c * F + (fc + 1) * P], xgT[:, k, c, :],
                                   start=(c == 0), stop=(c == DCH - 1))
                    o.then_inc(up_ps, 1)

            def down(i, k, n_in, first):
                pe.wait_ge(w2_in[k], 16 * n_in)
                if not first:
                    pe.wait_ge(y_ready, i)
                for half in range(2):
                    pe.wait_ge(act_ready, 2 * i + half + 1)
                    for f in range(FCH // 2):
                        fc = half * FCH // 2 + f
                        o = mm(ps[:, 7, 0:D], hid[:, k, fc, :], w2_sb[:, k, fc * D:(fc + 1) * D],
                               start=(fc == 0), stop=(fc == FCH - 1))
                o.then_inc(y_ps, 1)

            tileT(0, 0, 1)
            pe.wait_ge(b2_out, ROW_TILES)
            up(0, 0, 1)

            def step(i, k, n_in, n_next, first=False):
                tileT(i + 1, (k + 1) % RING, n_next)
                down(i, k, n_in, first)
                up(i + 1, (k + 1) % RING, n_next)

            step(0, 0, 1, 1, first=True)
            step(1, 1, 1, 1)
            step(2, 2, 1, 2)
            with pe.Fori(1, TILES // RING - 1) as r:
                for k in range(RING):
                    step(r * RING + k, k, r + 1, r + 1 if k < RING - 1 else r + 2)
            last = TILES // RING
            for k in range(RING - 1):
                step(TILES - RING + k, k, last, last)
            down(TILES - 1, RING - 1, last, False)


def kernel(**inputs):
    import concourse.bacc as _bacc
    from concourse.bass_utils import run_bass_kernel_spmd as _run

    a = {k: np.asarray(v) for k, v in inputs.items()}
    con = np.ascontiguousarray
    x_tok = a["x"].reshape(B, C, SIDE, PATCH, SIDE, PATCH).transpose(0, 2, 4, 3, 5, 1).reshape(TOK, PATCH_DIM)
    rows = np.concatenate([a["L0_tok_ln1_g"], a["L0_tok_ln1_b"], a["L0_tok_b"], a["L0_tok_ln2_g"], a["L0_tok_ln2_b"],
                           a["L0_attn_b_proj"], a["L0_ffn_rb"]])
    b_attn = a["L0_attn_b_attn"]
    bqk = b_attn[:2 * D].reshape(4, P).T
    bv = b_attn[2 * D:].reshape(PAIRS, 2, HD).transpose(1, 0, 2).reshape(2, PAIRS * HD)
    w1 = a["L0_ffn_w1"].transpose(0, 2, 1).reshape(E, DCH, P, F).transpose(0, 2, 1, 3).reshape(E, P, DCH * F)
    b1 = a["L0_ffn_b1"].reshape(E, FCH, P).transpose(0, 2, 1)
    w1 = np.concatenate([w1, b1], axis=2)
    w2 = a["L0_ffn_w2"].transpose(0, 2, 1).reshape(E, FCH, P, D).transpose(0, 2, 1, 3).reshape(E, P, FCH * D)
    arrays = {
        "x_tok": x_tok, "consts": const_table(), "rows": rows, "bqk": bqk, "bv": bv, "W": a["L0_tok_W"],
        "wattn": a["L0_attn_w_attn"], "wproj": a["L0_attn_w_proj"], "keysT": a["L0_ffn_keys"].T,
        "rwT": a["L0_ffn_rw"].T, "b2": a["L0_ffn_b2"], "w1": w1, "w2": w2,
    }
    nc = _bacc.Bacc("TRN2", target_bir_lowering=False, num_devices=1)
    fed, args = {}, []
    for name, v in arrays.items():
        v = con(v)
        fed[f"in_{name}"] = v
        args.append(nc.dram_tensor(f"in_{name}", v.shape, mybir.dt.from_np(v.dtype), kind="ExternalInput").ap())
    args.append(nc.dram_tensor("out_0", (TOK, D), mybir.dt.float32, kind="ExternalOutput").ap())
    build(nc, *args)
    r = _run(nc, [fed], core_ids=[0])
    return r.results[0]["out_0"].reshape(B, SEQ, D)
```

```python
import concourse.bass as bass
from concourse import mybir
from contextlib import ExitStack
import numpy as np

B, C, IMG, PATCH = 16, 3, 96, 16
SIDE = IMG // PATCH
SEQ = SIDE * SIDE
TOK = B * SEQ
P = 128
ROW_TILES = -(-TOK // P)
PAD_TOK = ROW_TILES * P
LAST_ROWS = TOK - (ROW_TILES - 1) * P
PATCH_DIM = C * PATCH * PATCH
PCH = PATCH_DIM // P
D = 256
DCH = D // P
HEADS, HD = 16, 16
HPC = P // HD
SLOT = 64
PAIRS = HEADS // 2
VW = 2 * HD + 2
HALF = TOK // 2
E, TOP_K, F = 16, 4, 1024
FCH = F // P
COPIES = TOK * TOP_K
E_TILES = ROW_TILES
OVERFLOW_TILES = (COPIES - E) // P
TILES = E + OVERFLOW_TILES
SURE_TILES = COPIES // P
RING = 6
SLACK = -TILES % RING
MAX_OVER = E_TILES - 1
EPS = 1e-5
W1_COLS = DCH * F + FCH
W_COLS = W1_COLS + FCH * D
AT_W, AT_SLOT, AT_TOK, ROW_W = D, D + TOP_K, D + 2 * TOP_K, D + 2 * TOP_K + 1
AT_LG = PAIRS * VW
AT_POS = AT_LG + 2 * E
GROUPS = [(0, 2), (2, 3), (3, 5)]

CONSTS = {}
_at = 0
for _name, _n in (("ident", P), ("mask", SEQ), ("before", P), ("headmask", HPC), ("iota_e", E), ("base", E),
                  ("over_at", MAX_OVER), ("tri", E * E), ("iota_o", OVERFLOW_TILES), ("pad_tok", 1),
                  ("tok", ROW_TILES), ("row", 1), ("prim_e", E), ("prim_t", E)):
    CONSTS[_name] = (_at, _n)
    _at += _n
CONST_COLS = _at
ROWS = {}
_at = 0
for _name, _n in (("tok_b", D), ("g2", D), ("b2", D), ("proj_b", D), ("rb", E)):
    ROWS[_name] = (_at, _n)
    _at += _n
ROW_COLS = _at
COLS = {}
_at = 0
for _name, _n in (("g1", PCH), ("b1", PCH), ("bqkv", 6)):
    COLS[_name] = (_at, _n)
    _at += _n
COL_COLS = _at


def const_table():
    t = np.zeros((P, CONST_COLS), np.float32)

    def put(name, value):
        at, n = CONSTS[name]
        t[:, at:at + n] = np.asarray(value, np.float32).reshape(-1, n)
    q = np.arange(P)[:, None] % SLOT
    k = np.arange(SEQ)[None, :]
    m = np.where(k > q, -np.log(np.maximum(k - q, 0) + 1.0), 0.0)
    m = np.where(k < q, -1e30, m)
    m[q[:, 0] >= SEQ] = 0.0
    rows = np.arange(P)[:, None]
    put("mask", m)
    put("ident", np.eye(P))
    put("before", rows < rows.T)
    put("headmask", rows // HD == np.arange(HPC)[None, :])
    put("iota_e", np.arange(E))
    put("base", np.arange(E) * E_TILES * P)
    put("over_at", (np.arange(MAX_OVER) + 1) * P)
    put("tri", (np.arange(E)[None, :] < np.arange(E)[:, None]).astype(np.float32).reshape(1, -1))
    put("iota_o", np.arange(OVERFLOW_TILES))
    put("pad_tok", TOK + rows)
    put("tok", rows + P * np.arange(ROW_TILES)[None, :])
    put("row", rows)
    put("prim_e", np.arange(E))
    put("prim_t", np.arange(E) * E_TILES)
    return t


def build(nc, x_tok, consts, rows, cols, W, wattn, wproj, keysT, rwT, b2, wexp, out):
    fp32 = mybir.dt.float32
    u32 = mybir.dt.uint32
    i32 = mybir.dt.int32
    ALU = mybir.AluOpType
    ACT = mybir.ActivationFunctionType
    X = mybir.AxisListType.X

    ctx = ExitStack()
    with ctx:
        def sb(name, shape, dt=fp32):
            return ctx.enter_context(nc.sbuf_tensor(name, shape, dt))

        def sem(name):
            return ctx.enter_context(nc.semaphore(name))

        x_sorted = nc.dram_tensor("x_sorted", (E * E_TILES * P, ROW_W), fp32, kind="Internal").ap()

        const = sb("const", [P, CONST_COLS])
        row = sb("row", [P, ROW_COLS])
        col = sb("col", [P, COL_COLS])

        def K(name):
            at, n = CONSTS[name]
            return const[:, at:at + n]

        def R(name):
            at, n = ROWS[name]
            return row[:, at:at + n]

        def CL(name):
            at, n = COLS[name]
            return col[:, at:at + n]

        ident = K("ident")
        W_sb = sb("W_sb", [P, PCH, D])
        wattn_sb = sb("wattn_sb", [P, DCH, 3 * D])
        wproj_sb = sb("wproj_sb", [P, DCH, D])
        keys_sb = sb("keys_sb", [P, DCH, E])
        rw_sb = sb("rw_sb", [P, DCH, E])
        kr = sb("kr", [P, DCH, E])
        nk2 = sb("nk2", [P, DCH, E])
        lbias = sb("lbias", [P, E])
        b2_sb = sb("b2_sb", [E, D])
        ones = sb("ones", [P, P])
        half_neg = sb("half_neg", [P, ROW_TILES])
        blank = sb("blank", [P, ROW_W])
        warm = sb("warm", [P, 2])

        space = sb("space", [P, 2 * PCH * PAD_TOK])
        x = space[:, 0:ROW_TILES * PATCH_DIM].rearrange("p (t n) -> p t n", t=ROW_TILES)
        xs = space[:, PCH * PAD_TOK:]
        xT = xs.rearrange("p (c n) -> p c n", c=PCH)
        PT = space[:, 0:PAIRS * P].rearrange("p (a n) -> p a n", n=P)
        OT = space[:, 1024:1024 + DCH * PAD_TOK].rearrange("p (c n) -> p c n", c=DCH)
        xaT = space[:, 2304:2304 + DCH * PAD_TOK].rearrange("p (c n) -> p c n", c=DCH)
        QT = xs[:, 0:DCH * PAD_TOK].rearrange("p (c n) -> p c n", c=DCH)
        KT = xs[:, 1280:1280 + DCH * TOK].rearrange("p (c n) -> p c n", c=DCH)
        S = xs[:, 2432:2432 + 2 * HEADS * SEQ].rearrange("p (u a s) -> p u a s", u=2, s=SEQ)

        mv = [sb(f"mv{i}", [P, ROW_TILES, 2]) for i in range(4)]
        stats = [sb(f"stats{i}", [P, ROW_TILES, 2, 6]) for i in range(4)]
        rstd = [sb(f"rstd{i}", [P, ROW_TILES]) for i in range(4)]
        bias_row = sb("bias_row", [P, D])
        h = sb("h", [P, ROW_TILES, D])
        xa = sb("xa", [P, ROW_TILES, ROW_W])
        kspace = sb("kspace", [P, DCH * B * HPC * SEQ])
        Kblk = kspace[:, :].rearrange("p (c b a s) -> p c b a s", c=DCH, b=B, a=HPC)
        shiftW = sb("shiftW", [P, D])
        gW = kspace[:, 0:PCH * D].rearrange("p (c n) -> p c n", c=PCH)
        Vblk = sb("Vblk", [P, B, PAIRS, VW])
        mx = sb("mx", [P, 2, HEADS])
        Pr = sb("Pr", [P, 2, HEADS, SLOT])
        rs = sb("rs", [P, HEADS])
        O = sb("O", [P, HEADS, HD])
        sq = sb("sq", [P, D])
        x2n = sb("x2n", [P, ROW_TILES])
        L = sb("L", [P, ROW_TILES, E])
        top = sb("top", [P, ROW_TILES, 8])
        topi = sb("topi", [P, ROW_TILES, 8], u32)
        topf = sb("topf", [P, ROW_TILES, TOP_K])
        dl = sb("dl", [P, ROW_TILES, TOP_K])
        hot = sb("hot", [P, ROW_TILES, TOP_K, E])
        tmp4 = sb("tmp4", [P, ROW_TILES, TOP_K, E])
        M = sb("M", [P, ROW_TILES, E])
        cum = sb("cum", [P, ROW_TILES, E])
        ew = sb("ew", [P, ROW_TILES, TOP_K])
        es = sb("es", [P, ROW_TILES])
        Wf = sb("Wf", [P, ROW_TILES, E])
        WT = sb("WT", [E, PAD_TOK])
        over = sb("over", [P, E, MAX_OVER])
        nover = sb("nover", [P, E])
        tri = sb("tri", [P, E, E])
        oend = sb("oend", [P, E])
        slot = sb("slot", [P, ROW_TILES, E])
        sloti = sb("sloti", [P, ROW_TILES, TOP_K], u32)
        ended = sb("ended", [P, OVERFLOW_TILES, E])
        endedn = sb("endedn", [P, OVERFLOW_TILES, E])
        tile_e = sb("tile_e", [P, TILES + SLACK])
        tile_t = sb("tile_t", [P, TILES + SLACK])
        past = sb("past", [P, OVERFLOW_TILES])
        mine = sb("mine", [P, TILES + SLACK])
        tile_ei = sb("tile_ei", [1, TILES + SLACK], i32)
        tile_ti = sb("tile_ti", [1, TILES + SLACK], i32)
        used_i = sb("used_i", [1, 1], i32)
        wslots = sb("wslots", [P, RING - 2, W_COLS])

        def wslot(k):
            at = (k - (RING - 2)) * W_COLS
            return wslots[:, k, :] if k < RING - 2 else kspace[:, at:at + W_COLS]

        xg = space[:, 0:RING * (ROW_W + 3)].rearrange("p (k n) -> p k n", k=RING)
        _o = RING * (ROW_W + 3)
        xgT = space[:, _o:_o + 2 * D].rearrange("p (k c n) -> p k c n", k=2, c=DCH)
        hid = space[:, _o + 2 * D:_o + 2 * D + 2 * F].rearrange("p (k f n) -> p k f n", k=2, f=FCH)
        ysb = space[:, _o + 2 * D + 2 * F:_o + 4 * D + 2 * F].rearrange("p (k n) -> p k n", k=2)
        eqw = sb("eqw", [P, 2, TOP_K])
        wrow = sb("wrow", [P, 2])

        ps = ctx.enter_context(nc.psum_tensor("ps", [P, 8, 512], fp32))

        x_in = [sem(f"x_in{t}") for t in range(ROW_TILES)]
        const_in, row_in, col_in, W_in, wattn_in, wproj_in, small_in = (
            sem(n) for n in ("const_in", "row_in", "col_in", "W_in", "wattn_in", "wproj_in", "small_in"))
        pad_zero, half_set, warm_set, ones_set, Vz, Pz, OTz, blank_set = (
            sem(n) for n in ("pad_zero", "half_set", "warm_set", "ones_set", "Vz", "Pz", "OTz", "blank_set"))
        dve_step, act_step, pool_step = sem("dve_step"), sem("act_step"), sem("pool_step")
        var_ready = [sem(f"var_ready{i}") for i in range(4)]
        rstd_ready = [sem(f"rstd_ready{i}") for i in range(4)]
        xn_ready, gw_ready, brow_ps, brow_ready, shift_ready = (sem(n) for n in ("xn_ready", "gw_ready", "brow_ps", "brow_ready", "shift_ready"))
        xT_ps, xT_ready, emb_ps, emb_out = sem("xT_ps"), sem("xT_ready"), sem("emb_ps"), sem("emb_out")
        h0_ready, h_ready, xa_ready = sem("h0_ready"), sem("h_ready"), sem("xa_ready")
        xaT_ps, xaT_ready = sem("xaT_ps"), sem("xaT_ready")
        qk_ps, q_ready, kt_ready = sem("qk_ps"), sem("q_ready"), sem("kt_ready")
        kblk0, kblk1, kblk1p = sem("kblk0"), sem("kblk1"), sem("kblk1p")
        v_ps, v_even, v_odd = sem("v_ps"), sem("v_even"), sem("v_odd")
        s_ps, s_out, mx_ready, s_sub, p_ready = (sem(n) for n in ("s_ps", "s_out", "mx_ready", "s_sub", "p_ready"))
        pt_ps, pt_ready, o_ps, o_ready, ot_ps, ot_ready = (
            sem(n) for n in ("pt_ps", "pt_ready", "o_ps", "o_ready", "ot_ps", "ot_ready"))
        hb_ready, pr_ps, pr_out, x2_ready = sem("hb_ready"), sem("pr_ps"), sem("pr_out"), sem("x2_ready")
        kr_ready, sq_ready, lb_ps = sem("kr_ready"), sem("sq_ready"), sem("lb_ps")
        x2T_ps, x2T_ready, lg_ps, m_ready, dl_ready, ew_ready = (
            sem(n) for n in ("x2T_ps", "x2T_ready", "lg_ps", "m_ready", "dl_ready", "ew_ready"))
        lg_read, pos_ps, pos_read, cnt_ps, wf_ready, wt_ps, wt_ready, b2_ps, b2_out = (
            sem(n) for n in ("lg_read", "pos_ps", "pos_read", "cnt_ps", "wf_ready", "wt_ps", "wt_ready", "b2_ps", "b2_out"))
        rows_ready, tables_ready, cum_ready = sem("rows_ready"), sem("tables_ready"), sem("cum_ready")
        blank_out, scattered, out_set, out_blank = (sem(n) for n in ("blank_out", "scattered", "out_set", "out_blank"))
        w1_in = [sem(f"w1_in{k}") for k in range(RING)]
        w2_in = [sem(f"w2_in{k}") for k in range(RING)]
        xg_in = [sem(f"xg_in{k}") for k in range(RING)]
        xgT_ps, xgT_ready, up_ps, act_ready, y_ps, y_ready, added = (
            sem(n) for n in ("xgT_ps", "xgT_ready", "up_ps", "act_ready", "y_ps", "y_ready", "added"))

        block = ctx.enter_context(nc.Block())

        def rows_of(t):
            return P if t < ROW_TILES - 1 else LAST_ROWS

        def last_attn(t1):
            return min(-(-(t1 * P) // SEQ), B) // 2 + min(-(-(t1 * P) // SEQ), B) % 2 - 1

        STEPS = B // 2 + 4

        def routed(t, lag):
            return max([t1 for t0, t1 in GROUPS if last_attn(t1) + lag <= t], default=0)

        def scores_bank(t, c):
            return (DCH * t + c) % 3

        def scatter(pool, t):
            pool.wait_ge(rows_ready, next(t1 for t0, t1 in GROUPS if t < t1))
            for k in range(TOP_K):
                pool.indirect_dma_start(
                    out=x_sorted[:, :], out_offset=bass.IndirectOffsetOnAxis(ap=sloti[0:rows_of(t), t, k:k + 1], axis=0),
                    in_=xa[0:rows_of(t), t, :], in_offset=None).then_inc(scattered, 16)

        def xa_bank(t):
            return 7 if t % 2 == 0 else 0

        def qk_bank(half, m):
            return (1 + m if half == 0 else 5 + m) % 8

        def pr_bank(t0):
            return 3 if t0 == GROUPS[2][0] else 7

        def v_bank(g):
            return 1 + g

        def xa_tok(ts):
            return xa[:, ts, AT_TOK:ROW_W].bitcast(u32)

        def emb_bank(t):
            return 4 + t % 3

        @block.sync
        def _(sp):
            sp.dma_start(x[:, 0, :], x_tok[0:P, :]).then_inc(x_in[0], 16)
            sp.dma_start(const[:, :], consts).then_inc(const_in, 16)
            sp.dma_start(x[:, 1, :], x_tok[P:2 * P, :]).then_inc(x_in[1], 16)
            sp.dma_start(W_sb[:, :, :], W.rearrange("(c p) n -> p c n", p=P)).then_inc(W_in, 16)
            for t in range(2, ROW_TILES):
                sp.dma_start(x[0:rows_of(t), t, :], x_tok[t * P:t * P + rows_of(t), :]).then_inc(x_in[t], 16)
            sp.dma_start(wattn_sb[:, :, :], wattn.rearrange("(c p) n -> p c n", p=P)).then_inc(wattn_in, 16)
            sp.dma_start(keys_sb[:, :, :], keysT.rearrange("(c p) n -> p c n", p=P)).then_inc(small_in, 16)
            sp.dma_start(rw_sb[:, :, :], rwT.rearrange("(c p) n -> p c n", p=P)).then_inc(small_in, 16)
            sp.dma_start(b2_sb[:, :], b2).then_inc(small_in, 16)
            sp.dma_start(wproj_sb[:, :, :], wproj.rearrange("(c p) n -> p c n", p=P)).then_inc(wproj_in, 16)
            sp.wait_ge(blank_set, 2)
            sp.dma_start(x_sorted.rearrange("(t p) n -> p t n", p=P),
                         blank[:, None, :].broadcast_to([P, E * E_TILES, ROW_W])).then_inc(blank_out, 16)
            sp.dma_start(out[TOK:TOK + P, :], blank[:, 0:D]).then_inc(out_blank, 16)
            for i in range(RING):
                if i == RING - 2:
                    sp.wait_ge(s_ps, B)
                sp.dma_start(wslot(i)[:, 0:W1_COLS], wexp[i, :, 0:W1_COLS]).then_inc(w1_in[i], 16)
                sp.dma_start(wslot(i)[:, W1_COLS:], wexp[i, :, W1_COLS:]).then_inc(w2_in[i], 16)
            sp.wait_ge(scattered, 16 * ROW_TILES * TOP_K)
            for i in range(RING):
                sp.dma_start(xg[:, i, 0:ROW_W], x_sorted[i * E_TILES * P:(i * E_TILES + 1) * P, :]).then_inc(xg_in[i], 16)
            for t in range(ROW_TILES):
                sp.wait_ge(b2_out, t + 1)
                sp.dma_start(out[t * P:t * P + rows_of(t), :], h[0:rows_of(t), t, :]).then_inc(out_set, 16)
            sp.wait_ge(tables_ready, 1)
            used = sp.value_load(used_i[0:1, 0:1], min_val=SURE_TILES, max_val=TILES)

            def tiles_from(r, k):
                i = r * RING + k
                with sp.If(i < used):
                    e = sp.value_load(tile_ei[0:1, bass.ds(i, 1)], min_val=0, max_val=E - 1)
                    at = sp.value_load(tile_ti[0:1, bass.ds(i, 1)], min_val=0, max_val=E * E_TILES - 1)
                    sp.wait_ge(act_ready, 2 * (i - (RING - 1)))
                    sp.dma_start(wslot(k)[:, 0:W1_COLS], wexp[bass.ds(e, 1), :, 0:W1_COLS].rearrange("o p n -> (o p) n")
                                 ).then_inc(w1_in[k], 16)
                    sp.wait_ge(y_ps, i - (RING - 1))
                    sp.dma_start(wslot(k)[:, W1_COLS:], wexp[bass.ds(e, 1), :, W1_COLS:].rearrange("o p n -> (o p) n")
                                 ).then_inc(w2_in[k], 16)
                    sp.wait_ge(added, 16 * (i - (RING - 1)))
                    sp.dma_start(xg[:, k, 0:ROW_W], x_sorted[bass.ds(at * P, P), :]).then_inc(xg_in[k], 16)
                    if k + 1 < RING:
                        tiles_from(r, k + 1)

            with sp.Fori(1, (TILES + SLACK) // RING) as r:
                tiles_from(r, 0)

        @block.gpsimd
        def _(pool):
            G = nc.gpsimd
            steps = [0]

            def link(ins):
                steps[0] += 1
                ins.then_inc(pool_step, 1)
                pool.wait_ge(pool_step, steps[0])

            G.memset(x[LAST_ROWS:P, ROW_TILES - 1, :], 0.0).then_inc(pad_zero, 1)
            pool.wait_ge(pad_zero, 1)
            G.memset(half_neg[:, :], -0.5).then_inc(half_set, 1)
            G.memset(blank[:, 0:AT_TOK], 0.0).then_inc(blank_set, 1)
            G.memset(Vblk[:, B // 2:, :, :], 0.0).then_inc(Vz, 1)

            def inverse_std(i, t0, t1):
                pool.wait_ge(var_ready[i], t1)
                link(G.tensor_scalar(rstd[i][:, t0:t1], mv[i][:, t0:t1, 1], EPS, None, ALU.add))
                G.tensor_tensor(rstd[i][:, t0:t1], rstd[i][:, t0:t1], half_neg[:, 0:t1 - t0], ALU.pow).then_inc(rstd_ready[i], t1 - t0)

            pool.wait_ge(half_set, 1)
            for s in range(ROW_TILES + 5):
                if s < ROW_TILES:
                    inverse_std(0, s, s + 1)
                if s == 0:
                    pool.wait_ge(const_in, 16)
                    G.tensor_copy(blank[:, AT_TOK:ROW_W].bitcast(u32), K("pad_tok")).then_inc(blank_set, 1)
                if 0 <= s - 4 < ROW_TILES:
                    inverse_std(1, s - 4, s - 3)
                if 0 <= s - 5 < ROW_TILES:
                    inverse_std(2, s - 5, s - 4)
                t = s - 4
                if 0 <= t < ROW_TILES:
                    if t == 0:
                        pool.wait_ge(row_in, 16)
                    pool.wait_ge(h0_ready, t + 1)
                    link(G.tensor_tensor(h[:, t, :], h[:, t, :], R("g2"), ALU.mult))
                    G.tensor_tensor(h[:, t, :], h[:, t, :], R("b2"), ALU.add).then_inc(h_ready, 1)
            pool.wait_ge(xT_ps, ROW_TILES)
            G.memset(OT[:, :, TOK:PAD_TOK], 0.0).then_inc(OTz, 1)
            G.memset(Pr[:, :, :, :], 0.0).then_inc(Pz, 1)
            pool.wait_ge(xa_ready, ROW_TILES)
            G.tensor_tensor(h[:, :, :], h[:, :, :],
                            R("proj_b")[:, None, :].broadcast_to([P, ROW_TILES, D]), ALU.add).then_inc(hb_ready, 1)

            def subtract_max(t):
                pool.wait_ge(mx_ready, t + 1)
                u = t % 2
                G.tensor_tensor(S[:, u, :, :], S[:, u, :, :],
                                mx[:, u, :, None].broadcast_to([P, HEADS, SEQ]), ALU.subtract).then_inc(s_sub, 1)

            def mask_heads(hh):
                return G.tensor_scalar(Kblk[:, 1, B // 2:, hh, :], KT[:, 1, HALF:].rearrange("p (b s) -> p b s", s=SEQ),
                                       K("headmask")[:, hh:hh + 1], None, ALU.mult)

            def inverse_stds(t):
                for t0, t1 in GROUPS:
                    if t == last_attn(t1) + 2:
                        inverse_std(3, t0, t1)

            pool.wait_ge(kt_ready, 4)
            for hh in range(HPC // 2, HPC):
                o = mask_heads(hh)
            o.then_inc(kblk1p, 1)
            for t in range(B // 2):
                subtract_max(t)
                inverse_stds(t)
            pool.wait_ge(blank_out, 16)
            scatter(pool, 0)
            inverse_std(3, *GROUPS[2])
            for t in range(1, ROW_TILES):
                scatter(pool, t)
            pool.wait_ge(out_set, 16 * ROW_TILES)
            pool.wait_ge(out_blank, 16)
            pool.wait_ge(tables_ready, 1)
            used = pool.value_load(used_i[0:1, 0:1], min_val=SURE_TILES, max_val=TILES)

            def add_rows(i, k):
                pool.indirect_dma_start(
                    out=out[:, :], out_offset=bass.IndirectOffsetOnAxis(ap=xg[:, k, AT_TOK:ROW_W].bitcast(u32), axis=0),
                    in_=ysb[:, k % 2, :], in_offset=None, compute_op=ALU.add).then_inc(added, 16)
                pool.wait_ge(added, 16 * (i + 1))

            pool.wait_ge(out_blank, 16)
            for i in range(RING):
                pool.wait_ge(y_ready, i + 1)
                add_rows(i, i)
            with pool.Fori(1, (TILES + SLACK) // RING) as r:
                for pair in range(0, RING, 2):
                    with pool.If(r * RING + pair < used):
                        for k in range(pair, pair + 2):
                            with pool.If(r * RING + k < used):
                                pool.wait_ge(y_ready, r * RING + k + 1)
                            with pool.If(r * RING + k < used):
                                add_rows(r * RING + k, k)

        @block.scalar
        def _(act):
            A = nc.scalar

            act.dma_start(col[:, :], cols).then_inc(col_in, 16)
            act.wait_ge(warm_set, 1)
            A.activation(warm[:, 0:1], warm[:, 0:1], ACT.Exp)
            act.wait_ge(col_in, 16)
            act.dma_start(row[:, :], rows.partition_broadcast(P)).then_inc(row_in, 16)
            act.wait_ge(W_in, 16)
            for c in range(PCH):
                o = A.activation(gW[:, c, :], W_sb[:, c, :], ACT.Copy, scale=CL("g1")[:, c:c + 1])
            o.then_inc(gw_ready, 1)

            def copy_xT(t):
                act.wait_ge(xT_ps, t + 1)
                bank = 2 * (t % 2)
                for u in range(2):
                    o = A.copy(xT[:, 3 * u:3 * u + 3, t * P:(t + 1) * P],
                               ps[:, bank + u, 0:3 * P].rearrange("p (c n) -> p c n", n=P))
                o.then_inc(xT_ready, 1)

            def copy_xaT(t):
                act.wait_ge(xaT_ps, t + 1)
                A.copy(xaT[:, :, t * P:(t + 1) * P],
                       ps[:, xa_bank(t), 0:D].rearrange("p (c n) -> p c n", c=DCH)).then_inc(xaT_ready, 1)

            for s in range(ROW_TILES):
                copy_xT(s)

            def take_qk(half):
                for m in range(4):
                    act.wait_ge(qk_ps, 4 * half + m + 1)
                    n = HALF + (32 * half if m < 2 else 0)
                    if m < 2:
                        A.activation(QT[:, m, half * HALF:half * HALF + n], ps[:, qk_bank(half, m), 0:n],
                                     ACT.Identity, bias=CL("bqkv")[:, m:m + 1]).then_inc(q_ready, 1)
                    else:
                        A.activation(KT[:, m - 2, half * HALF:half * HALF + n], ps[:, qk_bank(half, m), 0:n],
                                     ACT.Identity, bias=CL("bqkv")[:, m:m + 1]).then_inc(kt_ready, 1)

            def take_v(g):
                act.wait_ge(v_ps, g + 1)
                A.copy(Vblk[0:SLOT, 4 * g:4 * g + 4, :, 0:HD].rearrange("p b a n -> p (b a) n"),
                       ps[0:SLOT, v_bank(g), :].rearrange("p (b n) -> p b n", n=HD)).then_inc(v_even, 1)

            for t in range(3):
                copy_xaT(t)
            take_qk(0)
            act.wait_ge(Vz, 2)
            take_v(0)
            take_v(1)
            for t in range(3, ROW_TILES):
                copy_xaT(t)
            take_qk(1)
            take_v(2)
            take_v(3)
            act.wait_ge(Pz, 1)
            act.wait_ge(OTz, 1)

            def softmax_exp(t):
                act.wait_ge(s_sub, t + 1)
                if t >= 2:
                    act.wait_ge(pt_ps, t - 1)
                A.activation(Pr[:, t % 2, :, 0:SEQ], S[:, t % 2, :, :], ACT.Exp).then_inc(p_ready, 1)

            def copy_OT(t):
                act.wait_ge(ot_ps, t + 1)
                for c in range(DCH):
                    o = A.activation(OT[:, c, t * 2 * SEQ:(t + 1) * 2 * SEQ].rearrange("p (j s) -> p j s", s=SEQ),
                                     ps[:, 6, c * P:(c + 1) * P].rearrange("p (j s) -> p j s", s=SLOT)[:, :, 0:SEQ],
                                     ACT.Identity, bias=CL("bqkv")[:, 4 + c:5 + c])
                o.then_inc(ot_ready, 1)

            sqs = [0]

            def squares(t0, t1):
                act.wait_ge(x2T_ps, t1)
                A.copy(xaT[:, :, t0 * P:t1 * P].rearrange("p c n -> p c n"),
                       ps[:, 7, 0:(t1 - t0) * D].rearrange("p (c n) -> p c n", c=DCH)).then_inc(x2T_ready, t1 - t0)
                act.wait_ge(x2_ready, t1)
                for t in range(t0, t1):
                    o = A.activation(sq[:, :], xa[:, t, 0:D], ACT.Square, accum_out=x2n[:, t:t + 1])
                    sqs[0] += 1
                    if t == t1 - 1:
                        o.then_inc(sq_ready, 1)
                    else:
                        o.then_inc(act_step, 1)
                        act.wait_ge(act_step, sqs[0] - len([g for g in GROUPS if g[1] <= t]))

            def exp_w(t0, t1):
                act.wait_ge(dl_ready, t1)
                A.activation(ew[:, t0:t1, :], dl[:, t0:t1, :], ACT.Exp).then_inc(ew_ready, t1 - t0)

            def route(t):
                for t0, t1 in GROUPS:
                    if t == last_attn(t1) + 3:
                        exp_w(t0, t1)
                    if t == last_attn(t1) + 2:
                        squares(t0, t1)

            softmax_exp(0)
            for t in range(B // 2):
                act.wait_ge(pt_ps, t + 1)
                if t >= 1:
                    act.wait_ge(o_ps, t)
                for u in range(2):
                    o = A.copy(PT[:, 4 * u:4 * u + 4, :], ps[:, 3 + u, :].rearrange("p (a n) -> p a n", n=P))
                o.then_inc(pt_ready, 1)
                if t + 1 < B // 2:
                    softmax_exp(t + 1)
                if t >= 1:
                    copy_OT(t - 1)
                if t == B // 2 - 1:
                    copy_OT(t)
                route(t)
            exp_w(*GROUPS[1])
            squares(*GROUPS[2])
            exp_w(*GROUPS[2])
            A.activation(warm[:, 1:2], warm[:, 1:2], ACT.Gelu)
            act.wait_ge(wt_ps, 1)
            A.copy(WT[:, 0:4 * P], ps[0:E, 4, :])
            A.copy(WT[:, 4 * P:PAD_TOK], ps[0:E, 5, 0:P]).then_inc(wt_ready, 1)
            act.wait_ge(tables_ready, 1)
            used = act.value_load(used_i[0:1, 0:1], min_val=SURE_TILES, max_val=TILES)

            def gelu_tile(i, k):
                for half in range(2):
                    act.wait_ge(up_ps, 2 * i + half + 1)
                    for f in range(FCH // 2):
                        fc = half * FCH // 2 + f
                        o = A.activation(hid[:, k % 2, fc, :], ps[:, 2 * (k % 2) + half, f * P:(f + 1) * P], ACT.Gelu,
                                         bias=wslot(k)[:, DCH * F + fc:DCH * F + fc + 1])
                    o.then_inc(act_ready, 1)

            for i in range(RING):
                gelu_tile(i, i)

            def tiles_from(r, k):
                with act.If(r * RING + k < used):
                    gelu_tile(r * RING + k, k)
                    if k + 1 < RING:
                        tiles_from(r, k + 1)

            with act.Fori(1, (TILES + SLACK) // RING) as r:
                tiles_from(r, 0)

        @block.vector
        def _(dve):
            steps = [0]

            def link(ins):
                steps[0] += 1
                ins.then_inc(dve_step, 1)
                dve.wait_ge(dve_step, steps[0])

            V = nc.vector
            V.memset(warm[:, :], 0.0).then_inc(warm_set, 1)
            V.memset(ones[:, :], 1.0).then_inc(ones_set, 1)
            V.memset(Vblk[:, 0:B // 2, :, :], 0.0).then_inc(Vz, 1)

            def rows_stats(i, t0, t1, src, width):
                parts = -(-width // 512)
                n = width // parts
                for t in range(t0, t1):
                    for j in range(parts):
                        o = V.bn_stats(stats[i][:, t, j, :], src(t)[:, j * n:(j + 1) * n])
                link(o)
                for t in range(t0, t1):
                    V.bn_aggr(mv[i][:, t, :], stats[i][:, t, 0:parts, :].rearrange("p a b -> p (a b)")).then_inc(var_ready[i], 1)

            def norm(i, dst, src, t):
                return V.tensor_scalar(dst, src, mv[i][:, t, 0:1], rstd[i][:, t:t + 1], ALU.subtract, ALU.mult)

            for s in range(ROW_TILES + 6):
                if s < ROW_TILES:
                    dve.wait_ge(x_in[s], 16)
                    if s == ROW_TILES - 1:
                        dve.wait_ge(pad_zero, 1)
                    rows_stats(0, s, s + 1, lambda t: x[:, t, :], PATCH_DIM)
                t = s - 1
                if 0 <= t < ROW_TILES:
                    dve.wait_ge(rstd_ready[0], t + 1)
                    dve.wait_ge(var_ready[0], t + 1)
                    norm(0, x[:, t, :], x[:, t, :], t).then_inc(xn_ready, 1)
                if s == 2:
                    dve.wait_ge(col_in, 16)
                    dve.wait_ge(W_in, 16)
                    o = V.tensor_scalar(shiftW[:, :], W_sb[:, 0, :], CL("b1")[:, 0:1], None, ALU.mult)
                    for c in range(1, PCH):
                        link(o)
                        o = V.scalar_tensor_tensor(out=shiftW[:, :], in0=W_sb[:, c, :], scalar=CL("b1")[:, c:c + 1],
                                                   in1=shiftW[:, :], op0=ALU.mult, op1=ALU.add)
                    o.then_inc(shift_ready, 1)
                if s == 4:
                    dve.wait_ge(row_in, 16)
                    dve.wait_ge(brow_ps, 1)
                    V.tensor_tensor(bias_row[:, :], ps[:, 7, 0:D], R("tok_b"), ALU.add).then_inc(brow_ready, 1)
                    dve.wait_ge(brow_ready, 1)
                t = s - 4
                if 0 <= t < ROW_TILES:
                    dve.wait_ge(emb_ps, t + 1)
                    V.tensor_tensor(h[:, t, :], ps[:, emb_bank(t), 0:D], bias_row[:, :], ALU.add).then_inc(emb_out, 1)
                    dve.wait_ge(emb_out, t + 1)
                    rows_stats(1, t, t + 1, lambda t: h[:, t, :], D)
                t = s - 6
                if 0 <= t < ROW_TILES:
                    dve.wait_ge(rstd_ready[2], t + 1)
                    dve.wait_ge(var_ready[2], t + 1)
                    norm(2, xa[:, t, 0:D], h[:, t, :], t).then_inc(xa_ready, 1)
                t = s - 5
                if 0 <= t < ROW_TILES:
                    dve.wait_ge(h_ready, t + 1)
                    rows_stats(2, t, t + 1, lambda t: h[:, t, :], D)
                t = s - 4
                if 0 <= t < ROW_TILES:
                    dve.wait_ge(rstd_ready[1], t + 1)
                    dve.wait_ge(var_ready[1], t + 1)
                    norm(1, h[:, t, :], h[:, t, :], t).then_inc(h0_ready, 1)

            dve.wait_ge(Vz, 2)
            for j in range(2):
                V.memset(Vblk[j * SLOT:(j + 1) * SLOT, :, :, 2 * HD + j], 1.0).then_inc(Vz, 1)

            def mask_heads(c, half, heads=range(HPC)):
                for hh in heads:
                    o = V.tensor_scalar(Kblk[:, c, half * B // 2:(half + 1) * B // 2, hh, :],
                                        KT[:, c, half * HALF:(half + 1) * HALF].rearrange("p (b s) -> p b s", s=SEQ),
                                        K("headmask")[:, hh:hh + 1], None, ALU.mult)
                return o

            def take_v(g):
                dve.wait_ge(v_ps, g + 1)
                V.tensor_copy(Vblk[SLOT:P, 4 * g:4 * g + 4, :, HD:2 * HD].rearrange("p b a n -> p (b a) n"),
                              ps[SLOT:P, v_bank(g), :].rearrange("p (b n) -> p b n", n=HD)).then_inc(v_odd, 1)

            dve.wait_ge(const_in, 16)
            for c in range(DCH):
                dve.wait_ge(kt_ready, c + 1)
                o = mask_heads(c, 0)
            o.then_inc(kblk0, 1)
            take_v(0)
            take_v(1)
            dve.wait_ge(small_in, 16 * 3)
            V.scalar_tensor_tensor(out=kr[:, :, :], in0=keys_sb[:, :, :], scalar=2.0, in1=rw_sb[:, :, :],
                                   op0=ALU.mult, op1=ALU.add)
            V.scalar_tensor_tensor(out=nk2[:, :, :], in0=keys_sb[:, :, :], scalar=-1.0, in1=keys_sb[:, :, :],
                                   op0=ALU.mult, op1=ALU.mult).then_inc(kr_ready, 1)
            V.tensor_copy(xa_tok(slice(0, ROW_TILES)), K("tok")[:, :, None])
            V.memset(cum[:, 0, :], 0.0).then_inc(cum_ready, 1)
            dve.wait_ge(kt_ready, 3)
            mask_heads(0, 1)
            dve.wait_ge(kt_ready, 4)
            mask_heads(1, 1, range(HPC // 2)).then_inc(kblk1, 1)
            take_v(2)
            take_v(3)

            mask = K("mask")[:, None, :].broadcast_to([P, HPC, SEQ])

            def scores(t):
                u = t % 2
                if t >= 2:
                    dve.wait_ge(p_ready, t - 1)
                for c in range(DCH):
                    dve.wait_ge(s_ps, DCH * t + c + 1)
                    V.scalar_tensor_tensor(
                        out=S[:, u, c * HPC:(c + 1) * HPC, :],
                        in0=ps[:, scores_bank(t, c), 0:HPC * SEQ].rearrange("p (a s) -> p a s", s=SEQ),
                        scalar=HD ** -0.5, in1=mask, op0=ALU.mult, op1=ALU.add).then_inc(s_out, 1)
                dve.wait_ge(s_out, DCH * (t + 1))
                V.tensor_reduce(mx[:, u, :], S[:, u, :, :], X, ALU.max).then_inc(mx_ready, 1)

            def residual(t0, t1):
                for t in range(t0, t1):
                    if t == 0:
                        dve.wait_ge(hb_ready, 1)
                    dve.wait_ge(pr_ps, t + 1)
                    o = V.tensor_tensor(h[:, t, :], h[:, t, :], ps[:, pr_bank(t0), (t - t0) * D:(t - t0 + 1) * D], ALU.add)
                    o.then_inc(pr_out, 1)
                dve.wait_ge(pr_out, t1)
                rows_stats(3, t0, t1, lambda t: h[:, t, :], D)

            def normal(t0, t1):
                dve.wait_ge(rstd_ready[3], t1)
                dve.wait_ge(var_ready[3], t1)
                for t in range(t0, t1):
                    norm(3, xa[:, t, 0:D], h[:, t, :], t).then_inc(x2_ready, 1)

            def choose(t0, t1):
                n = t1 - t0
                ts = slice(t0, t1)
                dve.wait_ge(lg_ps, t1)
                dve.wait_ge(sq_ready, 1 + [g[0] for g in GROUPS].index(t0))
                V.tensor_tensor(L[:, ts, :], ps[:, 5, AT_LG:AT_LG + n * E].rearrange("p (t e) -> p t e", e=E),
                                lbias[:, None, :].broadcast_to([P, n, E]), ALU.add).then_inc(lg_read, n)
                dve.wait_ge(lg_read, t1)
                link(V.tensor_tensor(L[:, ts, :], L[:, ts, :], x2n[:, ts, None].broadcast_to([P, n, E]), ALU.subtract))
                for t in range(t0, t1):
                    o = V.max(top[:, t, :], L[:, t, :])
                link(o)
                for t in range(t0, t1):
                    o = V.max_index(topi[:, t, :], top[:, t, :], L[:, t, :])
                link(o)
                V.tensor_tensor(dl[:, ts, :], top[:, ts, 0:TOP_K],
                                top[:, ts, 0:1].broadcast_to([P, n, TOP_K]), ALU.subtract).then_inc(dl_ready, n)
                link(V.tensor_copy(topf[:, ts, :], topi[:, ts, 0:TOP_K]))
                for t in range(t0, t1):
                    o = V.tensor_tensor(hot[:, t, :, :], topf[:, t, :, None].broadcast_to([P, TOP_K, E]),
                                        K("iota_e")[:, None, :].broadcast_to([P, TOP_K, E]), ALU.is_equal)
                link(o)
                V.tensor_reduce(M[:, ts, :], hot[:, ts, :, :].rearrange("p t k e -> p t e k"), X, ALU.add).then_inc(m_ready, n)
                dve.wait_ge(m_ready, t1)
                for t in range(t0, min(t1, ROW_TILES - 1)):
                    dve.wait_ge(cum_ready, t + 1)
                    V.tensor_tensor(cum[:, t + 1, :], cum[:, t, :], M[:, t, :], ALU.add).then_inc(cum_ready, 1)

            def place(t0, t1):
                n = t1 - t0
                ts = slice(t0, t1)
                dve.wait_ge(ew_ready, t1)
                link(V.tensor_reduce(es[:, ts], ew[:, ts, :], X, ALU.add))
                link(V.reciprocal(es[:, ts], es[:, ts]))
                V.tensor_tensor(xa[:, ts, AT_W:AT_SLOT], ew[:, ts, :], es[:, ts, None].broadcast_to([P, n, TOP_K]), ALU.mult)
                dve.wait_ge(pos_ps, t1)
                V.tensor_tensor(slot[:, ts, :], ps[:, 5, AT_POS:AT_POS + n * E].rearrange("p (t e) -> p t e", e=E),
                                K("base")[:, None, :].broadcast_to([P, n, E]), ALU.add).then_inc(pos_read, n)
                dve.wait_ge(pos_read, t1)
                e4 = [P, n, TOP_K, E]
                link(V.tensor_tensor(tmp4[:, ts, :, :], hot[:, ts, :, :], slot[:, ts, None, :].broadcast_to(e4), ALU.mult))
                link(V.tensor_reduce(xa[:, ts, AT_SLOT:AT_TOK], tmp4[:, ts, :, :], X, ALU.add))
                V.tensor_copy(sloti[:, ts, :], xa[:, ts, AT_SLOT:AT_TOK]).then_inc(rows_ready, n)

            def route(t):
                for t0, t1 in GROUPS:
                    for lag, part in enumerate((residual, normal, choose, place)):
                        if t == last_attn(t1) + 1 + lag:
                            part(t0, t1)

            scores(0)
            scores(1)
            dve.wait_ge(lb_ps, 1)
            link(V.tensor_tensor(lbias[:, :], ps[:, 7, 480:480 + E], R("rb"), ALU.add))
            for t in range(B // 2):
                if t + 2 < B // 2:
                    scores(t + 2)
                dve.wait_ge(o_ps, t + 1)
                if t >= 1:
                    dve.wait_ge(ot_ps, t)
                o_pair = ps[:, 5, 0:PAIRS * VW].rearrange("p (a n) -> p a n", n=VW)
                link(V.reciprocal(rs[:, :].rearrange("p (a j) -> p a j", j=2), o_pair[:, :, 2 * HD:]))
                V.tensor_tensor(O[:, :, :].rearrange("p (a j) n -> p a j n", j=2),
                                o_pair[:, :, 0:2 * HD].rearrange("p a (j n) -> p a j n", n=HD),
                                rs[:, :].rearrange("p (a j) -> p a j", j=2)[:, :, :, None].broadcast_to([P, PAIRS, 2, HD]),
                                ALU.mult).then_inc(o_ready, 1)
                route(t)
            residual(*GROUPS[2])
            choose(*GROUPS[1])
            normal(*GROUPS[2])
            place(*GROUPS[1])
            choose(*GROUPS[2])
            place(*GROUPS[2])

            e4 = [P, ROW_TILES, TOP_K, E]
            link(V.tensor_tensor(tmp4[:, :, :, :], hot[:, :, :, :], xa[:, :, AT_W:AT_SLOT, None].broadcast_to(e4), ALU.mult))
            V.tensor_reduce(Wf[:, :, :], tmp4[:, :, :, :].rearrange("p t k e -> p t e k"), X, ALU.add).then_inc(wf_ready, 1)
            dve.wait_ge(cnt_ps, 1)
            link(V.tensor_tensor(over[:, :, :], ps[:, 6, 0:E, None].broadcast_to([P, E, MAX_OVER]),
                                 K("over_at")[:, None, :].broadcast_to([P, E, MAX_OVER]), ALU.is_gt))
            link(V.tensor_reduce(nover[:, :], over[:, :, :], X, ALU.add))
            link(V.tensor_tensor(tri[:, :, :], K("tri").rearrange("p (a b) -> p a b", b=E),
                                 nover[:, None, :].broadcast_to([P, E, E]), ALU.mult))
            link(V.tensor_reduce(oend[:, :], tri[:, :, :], X, ALU.add))
            link(V.tensor_tensor(oend[:, :], oend[:, :], nover[:, :], ALU.add))
            eo = [P, OVERFLOW_TILES, E]
            V.tensor_copy(tile_e[:, 0:E], K("prim_e"))
            V.tensor_copy(tile_t[:, 0:E], K("prim_t"))
            V.memset(tile_e[:, TILES:], 0.0)
            V.memset(tile_t[:, TILES:], 0.0)
            link(V.tensor_tensor(ended[:, :, :], oend[:, None, :].broadcast_to(eo),
                                 K("iota_o")[:, :, None].broadcast_to(eo), ALU.is_le))
            link(V.tensor_tensor(endedn[:, :, :], ended[:, :, :], nover[:, None, :].broadcast_to(eo), ALU.mult))
            over_e, over_t = tile_e[:, E:TILES], tile_t[:, E:TILES]
            V.tensor_reduce(over_e, ended[:, :, :], X, ALU.add)
            link(V.tensor_reduce(past[:, :], endedn[:, :, :], X, ALU.add))
            link(V.tensor_scalar(over_e, over_e, float(E - 1), None, ALU.min))
            V.scalar_tensor_tensor(out=over_t, in0=over_e, scalar=float(E_TILES), in1=K("iota_o"), op0=ALU.mult, op1=ALU.add)
            link(V.tensor_scalar(past[:, :], past[:, :], -1.0, None, ALU.add))
            link(V.tensor_tensor(over_t, over_t, past[:, :], ALU.subtract))
            link(V.tensor_scalar(over_t, over_t, float(E * E_TILES - 1), None, ALU.min))
            V.tensor_scalar(mine[:, :], tile_t[:, :], float(P), K("row"), ALU.mult, ALU.add)
            V.tensor_copy(tile_ei[:, :], tile_e[0:1, :])
            V.tensor_copy(tile_ti[:, :], tile_t[0:1, :])
            V.tensor_scalar(used_i[:, :], oend[0:1, E - 1:E], float(E), None, ALU.add).then_inc(tables_ready, 1)
            for t in range(ROW_TILES):
                dve.wait_ge(b2_ps, t + 1)
                V.tensor_tensor(h[:, t, :], h[:, t, :], ps[:, t % 4, 0:D], ALU.add).then_inc(b2_out, 1)

            dve.wait_ge(tables_ready, 1)
            used = dve.value_load(used_i[0:1, 0:1], min_val=SURE_TILES, max_val=TILES)

            def take_xT(i, k):
                dve.wait_ge(xgT_ps, i + 1)
                V.tensor_copy(xgT[:, k % 2, :, :], ps[:, 4, 0:D].rearrange("p (c n) -> p c n", n=P)).then_inc(xgT_ready, 1)

            def take_y(i, k, at):
                V.scalar_tensor_tensor(out=eqw[:, k % 2, :], in0=xg[:, k, AT_SLOT:AT_TOK], scalar=mine[:, at],
                                       in1=xg[:, k, AT_W:AT_SLOT], op0=ALU.is_equal, op1=ALU.mult).then_inc(dve_step, 1)
                dve.wait_ge(dve_step, steps[0] + 2 * i + 1)
                V.tensor_reduce(wrow[:, k % 2:k % 2 + 1], eqw[:, k % 2, :], X, ALU.add).then_inc(dve_step, 1)
                dve.wait_ge(dve_step, steps[0] + 2 * i + 2)
                dve.wait_ge(y_ps, i + 1)
                V.tensor_scalar(ysb[:, k % 2, :], ps[:, 5 + k % 2, 0:D], wrow[:, k % 2:k % 2 + 1], None, ALU.mult).then_inc(y_ready, 1)

            take_xT(0, 0)
            for i in range(RING):
                take_xT(i + 1, (i + 1) % RING)
                dve.wait_ge(xg_in[i], 16)
                if i >= 2:
                    dve.wait_ge(added, 16 * (i - 1))
                take_y(i, i, slice(i, i + 1))

            def tiles_from(r, k):
                i = r * RING + k
                with dve.If(i < used):
                    with dve.If(i + 1 < used):
                        take_xT(i + 1, (k + 1) % RING)
                    dve.wait_ge(xg_in[k], 16 * (r + 1))
                    dve.wait_ge(added, 16 * (i - 1))
                    take_y(i, k, bass.ds(i, 1))
                    if k + 1 < RING:
                        tiles_from(r, k + 1)

            with dve.Fori(1, (TILES + SLACK) // RING) as r:
                tiles_from(r, 0)

        @block.tensor
        def _(pe):
            mm = nc.tensor.matmul
            tr = nc.tensor.transpose

            def keep_warm(n):
                for _ in range(n):
                    mm(ps[:, 7, 0:P], ones[:, :], ones[:, :], start=True, stop=True)

            pe.wait_ge(ones_set, 1)
            keep_warm(12)
            pe.wait_ge(const_in, 16)

            def embed(t):
                pe.wait_ge(xT_ready, t + 1)
                if t == 0:
                    pe.wait_ge(gw_ready, 1)
                if t >= 3:
                    pe.wait_ge(emb_out, t - 2)
                for c in range(PCH):
                    o = mm(ps[:, emb_bank(t), 0:D], xT[:, c, t * P:(t + 1) * P], gW[:, c, :], start=(c == 0), stop=(c == PCH - 1))
                o.then_inc(emb_ps, 1)

            for t in range(ROW_TILES):
                pe.wait_ge(xn_ready, t + 1)
                if t >= 2:
                    pe.wait_ge(xT_ready, t - 1)
                for c in range(PCH):
                    o = tr(ps[:, 2 * (t % 2) + c // 3, (c % 3) * P:(c % 3 + 1) * P], x[:, t, c * P:(c + 1) * P], ident)
                o.then_inc(xT_ps, 1)
                if t == 0:
                    keep_warm(9)
                if t >= 1:
                    embed(t - 1)
                if t == 1:
                    pe.wait_ge(shift_ready, 1)
                    mm(ps[:, 7, 0:D], ones[:, :], shiftW[:, :], start=True, stop=True).then_inc(brow_ps, 1)
            embed(ROW_TILES - 1)

            def rows_T(t):
                pe.wait_ge(xa_ready, t + 1)
                if t == 0:
                    pe.wait_ge(brow_ready, 1)
                if t >= 2:
                    pe.wait_ge(xaT_ready, t - 1)
                for c in range(DCH):
                    o = tr(ps[:, xa_bank(t), c * P:(c + 1) * P], xa[:, t, c * P:(c + 1) * P], ident)
                o.then_inc(xaT_ps, 1)

            def queries_keys(half):
                for m in range(4):
                    n = HALF + (32 * half if m < 2 else 0)
                    for c in range(DCH):
                        o = mm(ps[:, qk_bank(half, m), 0:n], wattn_sb[:, c, m * P:(m + 1) * P],
                               xaT[:, c, half * HALF:half * HALF + n], start=(c == 0), stop=(c == DCH - 1))
                    o.then_inc(qk_ps, 1)

            def values(g):
                for b in range(4 * g, 4 * g + 4):
                    for c in range(DCH):
                        for j in range(2):
                            wv = wattn_sb[:, c, 2 * D:3 * D].rearrange("p (a j n) -> p a j n", j=2, n=HD)[:, :, j, :]
                            o = mm(ps[j * SLOT:(j + 1) * SLOT, v_bank(g), (b % 4) * P:(b % 4 + 1) * P],
                                   xaT[:, c, b * SEQ:b * SEQ + SLOT], wv, start=(c == 0), stop=(c == DCH - 1))
                o.then_inc(v_ps, 1)

            for t in range(3):
                rows_T(t)
            pe.wait_ge(wattn_in, 16)
            pe.wait_ge(xaT_ready, 3)
            pe.wait_ge(emb_out, ROW_TILES)
            queries_keys(0)
            pe.wait_ge(q_ready, 2)
            values(0)
            values(1)
            for t in range(3, ROW_TILES):
                rows_T(t)
            pe.wait_ge(xaT_ready, ROW_TILES)
            queries_keys(1)
            pe.wait_ge(kt_ready, 2)
            values(2)
            values(3)

            def scores(t):
                pe.wait_ge(q_ready, 2 if t < 3 else 4)
                if t == 0:
                    pe.wait_ge(kblk0, 1)
                    pe.wait_ge(kt_ready, 4)
                    pe.wait_ge(v_even, 2)
                    pe.wait_ge(v_odd, 2)
                if t == B // 4:
                    pe.wait_ge(kblk1, 1)
                    pe.wait_ge(kblk1p, 1)
                for c in range(DCH):
                    if DCH * t + c >= 3:
                        pe.wait_ge(s_out, DCH * t + c - 2)
                    for j in range(2):
                        b = 2 * t + j
                        o = mm(ps[j * SLOT:(j + 1) * SLOT, scores_bank(t, c), 0:HPC * SEQ],
                               QT[:, c, b * SEQ:b * SEQ + SLOT], Kblk[:, c, b, :, :].rearrange("p a s -> p (a s)"),
                               start=True, stop=True)
                    o.then_inc(s_ps, 1)

            def probs_T(t):
                pe.wait_ge(p_ready, t + 1)
                if t == 0:
                    pe.wait_ge(v_even, 4)
                    pe.wait_ge(v_odd, 4)
                if t >= 1:
                    pe.wait_ge(pt_ready, t)
                for a in range(PAIRS):
                    o = tr(ps[:, 3 + a // 4, (a % 4) * P:(a % 4 + 1) * P],
                           Pr[:, t % 2, 2 * a:2 * a + 2, :].rearrange("p a s -> p (a s)"), ident)
                o.then_inc(pt_ps, 1)

            def bank5_free(t):
                if t >= 1:
                    pe.wait_ge(o_ready, min(t, B // 2))
                if routed(t - 1, 3):
                    pe.wait_ge(lg_read, routed(t - 1, 3))
                if routed(t - 1, 4):
                    pe.wait_ge(pos_read, routed(t - 1, 4))

            def attend(t):
                pe.wait_ge(pt_ready, t + 1)
                if t == 0:
                    pe.wait_ge(Vz, 4)
                bank5_free(t)
                for a in range(PAIRS):
                    for j in range(2):
                        o = mm(ps[j * SLOT:(j + 1) * SLOT, 5, a * VW:(a + 1) * VW],
                               PT[:, a, j * SLOT:(j + 1) * SLOT], Vblk[:, 2 * t + j, a, :], start=True, stop=True)
                o.then_inc(o_ps, 1)

            def out_T(t):
                pe.wait_ge(o_ready, t + 1)
                if t >= 1:
                    pe.wait_ge(ot_ready, t)
                for c in range(DCH):
                    o = tr(ps[:, 6, c * P:(c + 1) * P], O[:, c * HPC:(c + 1) * HPC, :].rearrange("p a n -> p (a n)"), ident)
                o.then_inc(ot_ps, 1)

            def project(t0, t1):
                pe.wait_ge(wproj_in, 16)
                pe.wait_ge(ot_ready, last_attn(t1) + 1)
                if pr_bank(t0) == 3:
                    pe.wait_ge(pt_ready, B // 2)
                elif t0 > 0:
                    pe.wait_ge(x2T_ready, t0)
                for t in range(t0, t1):
                    for c in range(DCH):
                        o = mm(ps[:, pr_bank(t0), (t - t0) * D:(t - t0 + 1) * D], OT[:, c, t * P:(t + 1) * P], wproj_sb[:, c, :],
                               start=(c == 0), stop=(c == DCH - 1))
                    if t == t1 - 1:
                        o.then_inc(pr_ps, t1 - t0)

            def rows2_T(t0, t1):
                pe.wait_ge(x2_ready, t1)
                n = (t1 - t0) * P
                for c in range(DCH):
                    for t in range(t0, t1):
                        at = c * n + (t - t0) * P
                        o = tr(ps[:, 7, at:at + P], xa[:, t, c * P:(c + 1) * P], ident)
                o.then_inc(x2T_ps, t1 - t0)

            def logits(t0, t1):
                pe.wait_ge(x2T_ready, t1)
                for t in range(t0, t1):
                    for c in range(DCH):
                        o = mm(ps[:, 5, AT_LG + (t - t0) * E:AT_LG + (t - t0 + 1) * E], xaT[:, c, t * P:(t + 1) * P], kr[:, c, :],
                               start=(c == 0), stop=(c == DCH - 1))
                o.then_inc(lg_ps, t1 - t0)

            def positions(t0, t1):
                pe.wait_ge(m_ready, t1)
                pe.wait_ge(cum_ready, t1)
                at = ps[:, 5, AT_POS:AT_POS + (t1 - t0) * E]
                mm(at, ones[:, :], cum[:, t0:t1, :].rearrange("p t e -> p (t e)"), start=True, stop=False)
                mm(at, K("before"), M[:, t0:t1, :].rearrange("p t e -> p (t e)"), start=False, stop=True).then_inc(pos_ps, t1 - t0)

            def route_small(t):
                for t0, t1 in GROUPS:
                    a = last_attn(t1)
                    if t == a + 4:
                        bank5_free(t)
                        positions(t0, t1)
                    if t == a + 3:
                        bank5_free(t)
                        logits(t0, t1)

            def route(t):
                for t0, t1 in GROUPS:
                    a = last_attn(t1)
                    if t == a + 1:
                        project(t0, t1)
                    if t == a + 2:
                        rows2_T(t0, t1)

            scores(0)
            scores(1)
            pe.wait_ge(kr_ready, 1)
            pe.wait_ge(ones_set, 1)
            for c in range(DCH):
                o = mm(ps[:, 7, 480:480 + E], ones[:, :], nk2[:, c, :], start=(c == 0), stop=(c == DCH - 1))
            o.then_inc(lb_ps, 1)
            for t in range(B // 2):
                probs_T(t)
                if t >= 1:
                    out_T(t - 1)
                if t + 2 < B // 2:
                    scores(t + 2)
                route_small(t)
                attend(t)
                if t == B // 2 - 1:
                    out_T(t)
                    project(*GROUPS[2])
                route(t)
            pe.wait_ge(o_ready, B // 2)
            pe.wait_ge(pos_read, GROUPS[0][1])
            logits(*GROUPS[1])
            pe.wait_ge(lg_read, GROUPS[1][1])
            positions(*GROUPS[1])
            rows2_T(*GROUPS[2])
            pe.wait_ge(pos_read, GROUPS[1][1])
            logits(*GROUPS[2])
            pe.wait_ge(lg_read, GROUPS[2][1])
            positions(*GROUPS[2])
            pe.wait_ge(pos_read, GROUPS[2][1])
            mm(ps[:, 6, 0:E], ones[:, :], cum[:, ROW_TILES - 1, :], start=True, stop=False)
            mm(ps[:, 6, 0:E], ones[0:LAST_ROWS, :], M[0:LAST_ROWS, ROW_TILES - 1, :], start=False, stop=True).then_inc(cnt_ps, 1)
            keep_warm(2)
            pe.wait_ge(wf_ready, 1)
            for t in range(ROW_TILES):
                o = tr(ps[0:E, 4 + t // 4, (t % 4) * P:(t % 4 + 1) * P], Wf[:, t, :], ident)
            o.then_inc(wt_ps, 1)
            keep_warm(2)
            pe.wait_ge(wt_ready, 1)
            for t in range(ROW_TILES):
                if t >= 4:
                    pe.wait_ge(b2_out, t - 3)
                mm(ps[:, t % 4, 0:D], WT[:, t * P:(t + 1) * P], b2_sb[:, :], start=True, stop=True).then_inc(b2_ps, 1)
            keep_warm(14)
            pe.wait_ge(tables_ready, 1)
            used = pe.value_load(used_i[0:1, 0:1], min_val=SURE_TILES, max_val=TILES)

            def tile_T(i, k, n_in):
                pe.wait_ge(xg_in[k], 16 * n_in)
                for c in range(DCH):
                    o = tr(ps[:, 4, c * P:(c + 1) * P], xg[:, k, c * P:(c + 1) * P], ident)
                o.then_inc(xgT_ps, 1)

            def up(i, k, n_in):
                pe.wait_ge(w1_in[k], 16 * n_in)
                pe.wait_ge(xgT_ready, i + 1)
                for half in range(2):
                    for f in range(FCH // 2):
                        fc = half * FCH // 2 + f
                        for c in range(DCH):
                            o = mm(ps[:, 2 * (k % 2) + half, f * P:(f + 1) * P],
                                   wslot(k)[:, c * F + fc * P:c * F + (fc + 1) * P], xgT[:, k % 2, c, :],
                                   start=(c == 0), stop=(c == DCH - 1))
                    o.then_inc(up_ps, 1)

            def down(i, k, n_in, reuse):
                pe.wait_ge(w2_in[k], 16 * n_in)
                if reuse:
                    pe.wait_ge(y_ready, i - 1)
                for half in range(2):
                    pe.wait_ge(act_ready, 2 * i + half + 1)
                    for f in range(FCH // 2):
                        fc = half * FCH // 2 + f
                        o = mm(ps[:, 5 + k % 2, 0:D], hid[:, k % 2, fc, :], wslot(k)[:, W1_COLS + fc * D:W1_COLS + (fc + 1) * D],
                               start=(fc == 0), stop=(fc == FCH - 1))
                o.then_inc(y_ps, 1)

            tile_T(0, 0, 1)
            pe.wait_ge(b2_out, ROW_TILES)
            up(0, 0, 1)
            for i in range(RING):
                nxt = (i + 1) // RING + 1
                tile_T(i + 1, (i + 1) % RING, nxt)
                down(i, i, 1, i >= 2)
                up(i + 1, (i + 1) % RING, nxt)

            def tiles_from(r, k):
                i = r * RING + k
                nxt = r + 1 if k < RING - 1 else r + 2
                with pe.If(i < used):
                    with pe.If(i + 1 < used):
                        tile_T(i + 1, (k + 1) % RING, nxt)
                    down(i, k, r + 1, True)
                    with pe.If(i + 1 < used):
                        up(i + 1, (k + 1) % RING, nxt)
                        if k + 1 < RING:
                            tiles_from(r, k + 1)

            with pe.Fori(1, (TILES + SLACK) // RING) as r:
                tiles_from(r, 0)


def kernel(**inputs):
    import concourse.bacc as _bacc
    from concourse.bass_utils import run_bass_kernel_spmd as _run

    a = {k: np.asarray(v) for k, v in inputs.items()}
    con = np.ascontiguousarray
    x_tok = a["x"].reshape(B, C, SIDE, PATCH, SIDE, PATCH).transpose(0, 2, 4, 3, 5, 1).reshape(TOK, PATCH_DIM)
    rows = np.concatenate([a["L0_tok_b"], a["L0_tok_ln2_g"], a["L0_tok_ln2_b"], a["L0_attn_b_proj"], a["L0_ffn_rb"]])
    cols = np.concatenate([a["L0_tok_ln1_g"].reshape(PCH, P), a["L0_tok_ln1_b"].reshape(PCH, P),
                           a["L0_attn_b_attn"].reshape(6, P)]).T
    w1 = a["L0_ffn_w1"].transpose(0, 2, 1).reshape(E, DCH, P, F).transpose(0, 2, 1, 3).reshape(E, P, DCH * F)
    b1 = a["L0_ffn_b1"].reshape(E, FCH, P).transpose(0, 2, 1)
    w2 = a["L0_ffn_w2"].transpose(0, 2, 1).reshape(E, FCH, P, D).transpose(0, 2, 1, 3).reshape(E, P, FCH * D)
    arrays = {
        "x_tok": x_tok, "consts": const_table(), "rows": rows, "cols": cols, "W": a["L0_tok_W"],
        "wattn": a["L0_attn_w_attn"], "wproj": a["L0_attn_w_proj"], "keysT": a["L0_ffn_keys"].T,
        "rwT": a["L0_ffn_rw"].T, "b2": a["L0_ffn_b2"], "wexp": np.concatenate([w1, b1, w2], axis=2),
    }
    nc = _bacc.Bacc("TRN2", target_bir_lowering=False, num_devices=1)
    fed, args = {}, []
    for name, v in arrays.items():
        v = con(v)
        fed[f"in_{name}"] = v
        args.append(nc.dram_tensor(f"in_{name}", v.shape, mybir.dt.from_np(v.dtype), kind="ExternalInput").ap())
    args.append(nc.dram_tensor("out_0", (TOK + P, D), mybir.dt.float32, kind="ExternalOutput").ap())
    build(nc, *args)
    r = _run(nc, [fed], core_ids=[0])
    return r.results[0]["out_0"][:TOK].reshape(B, SEQ, D)
```
